# Optimizing a Trainium2 kernel written in Bass

```python
import numpy as np
import jax
import jax.numpy as jnp

def _softmax(x, axis=-1):
    return jax.nn.softmax(x, axis=axis)
def _gelu(x):
    return jax.nn.gelu(x, approximate=True)
def _silu(x):
    return jax.nn.silu(x)
def _sigmoid(x):
    return jax.nn.sigmoid(x)
def _layernorm(x, axis=-1, eps=1e-5):
    m = jnp.mean(x, axis=axis, keepdims=True)
    v = jnp.var(x, axis=axis, keepdims=True)
    return (x - m) / jnp.sqrt(v + eps)
def _scatter_add(tgt, idx, src, axis=0):
    return tgt.at[idx].add(src)
def _segment_sum(src, seg, n):
    return jax.ops.segment_sum(src, seg, n)

kernel_name = 'mk_adj_resnorm_d2_adj_64_948a06'

def setup_inputs(seed: int = 0):
    np.random.seed(seed)
    _w = jnp.asarray
    def _rec_inputs():
        import jax
        import jax.numpy as jnp
        _gk = jax.random.key(seed)
        x = -0.006082 + 1.001 * jax.random.normal(jax.random.fold_in(_gk, 1), (128, 128, 64), jnp.float32)
        _w = (1.0 + jnp.arange(128, dtype=jnp.float32)) ** -0.5
        _w = _w / _w.mean()
        _pij = jnp.clip(0.0625 * _w[:, None] * _w[None, :], 0.0, 1.0)
        _a = jax.random.uniform(jax.random.fold_in(_gk, 2), (128, 128, 128)) < _pij
        _a = jnp.logical_or(_a, jnp.swapaxes(_a, -1, -2))
        _a = jnp.logical_or(_a, jnp.eye(128, dtype=bool))
        _af = _a.astype(jnp.float32)
        _af = _af * jax.random.uniform(jax.random.fold_in(_gk, 3), (128, 128, 128), jnp.float32, 0.05, 4.42607)
        adj = _af
        return x, adj
    x, adj = _rec_inputs()
    def _L0_gnn_setup():
        import jax, jax.numpy as jnp
        import numpy as np
        key = jax.random.key(seed)
        ks = jax.random.split(key, 6)
        B, N, F, H, O = (2, 512, 64, 192, 64)
        x = jax.random.normal(ks[0], (B, N, F), dtype=jnp.float32)
        adj = jax.random.normal(ks[1], (B, N, N), dtype=jnp.float32)
        W1 = jax.random.normal(ks[2], (2 * F, H), dtype=jnp.float32) * (1.0 / np.sqrt(2 * F))
        b1 = jax.random.normal(ks[3], (H,), dtype=jnp.float32) * 0.02
        W2 = jax.random.normal(ks[4], (H, O), dtype=jnp.float32) * (1.0 / np.sqrt(H))
        b2 = jax.random.normal(ks[5], (O,), dtype=jnp.float32) * 0.02
        return {'x': x, 'adj': adj, 'W1': W1, 'b1': b1, 'W2': W2, 'b2': b2}
    _L0_gnn_all = _L0_gnn_setup()
    _L0_gnn_in = {k: v for k, v in _L0_gnn_all.items() if k in ('W1', 'b1', 'W2', 'b2', )}
    del _L0_gnn_all

    def _L1_gnn_setup():
        import jax, jax.numpy as jnp
        import numpy as np
        B, N, H = (4, 4096, 64)
        key = jax.random.key(seed)
        ks = jax.random.split(key, 12)
        s = 1.0 / np.sqrt(H)
        h = jax.random.normal(ks[0], (B, N, H), dtype=jnp.float32)
        A = jax.random.uniform(ks[1], (B, N, N), dtype=jnp.float32)
        W1 = jax.random.normal(ks[2], (H, H), dtype=jnp.float32) * s
        b1 = jnp.zeros((H,), dtype=jnp.float32)
        W2 = jax.random.normal(ks[3], (H, H), dtype=jnp.float32) * s
        b2 = jnp.zeros((H,), dtype=jnp.float32)
        W_ih = jax.random.normal(ks[4], (3 * H, H), dtype=jnp.float32) * s
        b_ih = jnp.zeros((3 * H,), dtype=jnp.float32)
        W_hh = jax.random.normal(ks[5], (3 * H, H), dtype=jnp.float32) * s
        b_hh = jnp.zeros((3 * H,), dtype=jnp.float32)
        return {'h': h, 'A': A, 'W1': W1, 'b1': b1, 'W2': W2, 'b2': b2, 'W_ih': W_ih, 'b_ih': b_ih, 'W_hh': W_hh, 'b_hh': b_hh}
    _L1_gnn_all = _L1_gnn_setup()
    _L1_gnn_in = {k: v for k, v in _L1_gnn_all.items() if k in ('W1', 'b1', 'W2', 'b2', 'W_ih', 'b_ih', 'W_hh', 'b_hh', )}
    del _L1_gnn_all

    return {
        "x": x,
        "adj": adj,
        "L0_gnn_W1": _L0_gnn_in["W1"],
        "L0_gnn_b1": _L0_gnn_in["b1"],
        "L0_gnn_W2": _L0_gnn_in["W2"],
        "L0_gnn_b2": _L0_gnn_in["b2"],
        "L1_gnn_W1": _L1_gnn_in["W1"],
        "L1_gnn_b1": _L1_gnn_in["b1"],
        "L1_gnn_W2": _L1_gnn_in["W2"],
        "L1_gnn_b2": _L1_gnn_in["b2"],
        "L1_gnn_W_ih": _L1_gnn_in["W_ih"],
        "L1_gnn_b_ih": _L1_gnn_in["b_ih"],
        "L1_gnn_W_hh": _L1_gnn_in["W_hh"],
        "L1_gnn_b_hh": _L1_gnn_in["b_hh"],
    }

def reference(x, adj, L0_gnn_W1, L0_gnn_b1, L0_gnn_W2, L0_gnn_b2, L1_gnn_W1, L1_gnn_b1, L1_gnn_W2, L1_gnn_b2, L1_gnn_W_ih, L1_gnn_b_ih, L1_gnn_W_hh, L1_gnn_b_hh):
    import jax
    import jax.numpy as jnp
    def _L0_gnn_ref(x, adj, W1, b1, W2, b2):
        import jax, jax.numpy as jnp
        import numpy as np
        F = x.shape[-1]
        mask = (adj > 0.0).astype(x.dtype)
        W1a, W1b = (W1[:F], W1[F:])
        xj_proj = x @ W1a
        diff = x[:, :, None, :] - x[:, None, :, :]
        h = jax.nn.relu(xj_proj[:, :, None, :] + diff @ W1b + b1)
        hm = jnp.einsum('bjkh,bjk->bjh', h, mask)
        deg = jnp.sum(mask, axis=-1)
        return hm @ W2 + deg[..., None] * b2

    def _L1_gnn_ref(h, A, W1, b1, W2, b2, W_ih, b_ih, W_hh, b_hh):
        import jax, jax.numpy as jnp
        import numpy as np
        B, N, H = (4, 4096, 64)
        m = jax.nn.relu(jnp.einsum('bnh,hk->bnk', h, W1) + b1)
        m = jax.nn.relu(jnp.einsum('bnh,hk->bnk', m, W2) + b2)
        msg = jax.nn.relu(jnp.einsum('bij,bjh->bih', A, m))
        gi = jnp.einsum('bnh,gh->bng', msg, W_ih) + b_ih
        gh = jnp.einsum('bnh,gh->bng', h, W_hh) + b_hh
        i_r, i_z, i_n = jnp.split(gi, 3, axis=-1)
        h_r, h_z, h_n = jnp.split(gh, 3, axis=-1)
        r = jax.nn.sigmoid(i_r + h_r)
        z = jax.nn.sigmoid(i_z + h_z)
        n = jnp.tanh(i_n + r * h_n)
        return (1.0 - z) * n + z * h

    x = _layernorm(x + _L0_gnn_ref(x, adj, L0_gnn_W1, L0_gnn_b1, L0_gnn_W2, L0_gnn_b2), axis=-1)
    x = _layernorm(x + _L1_gnn_ref(x, adj, L1_gnn_W1, L1_gnn_b1, L1_gnn_W2, L1_gnn_b2, L1_gnn_W_ih, L1_gnn_b_ih, L1_gnn_W_hh, L1_gnn_b_hh), axis=-1)
    return x


_drawn_inputs = setup_inputs


def setup_inputs(seed=0):
    import zlib

    import numpy as np

    out = dict(_drawn_inputs(seed))
    spreads = {'L1_gnn_b1': (0.0, 0.1),
     'L1_gnn_b2': (0.0, 0.1),
     'L1_gnn_b_ih': (0.0, 0.8),
     'L1_gnn_b_hh': (0.0, 0.8)}
    factors = {'L0_gnn_b1': 3.024}
    for name, (base, spread) in spreads.items():
        noise = np.random.default_rng([zlib.crc32(name.encode()), seed]).standard_normal(out[name].shape)
        drawn = base * np.exp(spread * noise) if base else spread * noise
        out[name] = jnp.asarray(drawn.astype(out[name].dtype))
    for name, factor in factors.items():
        out[name] = (out[name] * factor).astype(out[name].dtype)
    return out
```

```python
from contextlib import ExitStack

import numpy as np

import concourse.bass as bass
from concourse import mybir

F32 = mybir.dt.float32
BF16 = mybir.dt.bfloat16
I32 = mybir.dt.int32
ALU = mybir.AluOpType
ACT = mybir.ActivationFunctionType
AX = mybir.AxisListType

NB = 128
N = 128
F = 64
H = 192
GB = 8
NG = NB // GB
PG = GB // 2
NP = NB // 2
C = 12
NT = 2
NROW = NT * 128
NTH = 11
EPS = 1e-5
LIMIT = NROW

CI = 0
CTX = CI + 128
CTI = CTX + 128
CRS = CTI + 128
CIO = CRS + GB * 128
CTH = CIO + 512
CKV = CTH + NTH
CSL = CKV + 4
NC = CSL + 3


def constants():
    c = np.zeros((128, NC), np.float32)
    i = np.arange(128)
    c[:, CI:CI + 128] = np.eye(128)
    c[:, CTX:CTX + 128] = i[:, None] < i[None, :]
    c[:, CTI:CTI + 128] = i[:, None] <= i[None, :]
    c[:, CRS:CRS + GB * 128] = (np.arange(GB * 128) % 128 != 0)[None, :]
    c[:, CIO:CIO + 512] = (np.arange(512) % 256)[None, :]
    c[:, CTH:CTH + NTH] = (C * np.arange(NTH))[None, :]
    for t in range(4):
        c[:, CKV + t] = C * (i + 128 * (t % 2)) + C
    c[:, CSL:CSL + 3] = i[:, None] == np.arange(3)[None, :]
    return c


class Queues:

    def __init__(self, sem):
        self.sem = sem
        self.sems = {}
        self.value = {}
        self.lists = {e: [] for e in ("tensor", "vector", "scalar", "gpsimd", "sync")}

    def put(self, engine, make, waits=(), done=None, n=1):
        token = None
        if done:
            if done not in self.sems:
                self.sems[done] = self.sem(done)
                self.value[done] = 0
            self.value[done] += n
            token = (done, self.value[done])
        self.lists[engine].append((make, [w for w in waits if w], done, n))
        return token

    def run(self, name, engine):
        seen = {}
        for make, waits, done, n in self.lists[name]:
            need = {}
            for s, v in waits:
                if v > seen.get(s, 0):
                    need[s] = max(need.get(s, 0), v)
            for s, v in need.items():
                engine.wait_ge(self.sems[s], v)
                seen[s] = v
            last = make(engine)
            if done:
                last.then_inc(self.sems[done], n)


def build(nc, adj, adjt, x, xt, w1, w1bt, b1, w2, b2, w1g, b1g, w2g, b2g, wih, bih, whh, bhh, cst, out):
    ctx = ExitStack()
    with ctx:
        def sb(name, shape, dt=F32):
            return ctx.enter_context(nc.sbuf_tensor(name, shape, dt))

        q = Queues(lambda name: ctx.enter_context(nc.semaphore(name)))
        T = {}

        def put(*args, **kw):
            return q.put(*args, **kw)

        def tk(name, i):
            return T.get((name, i))

        cs = sb("cs", [128, NC])
        idb = sb("idb", [128, 128], BF16)
        trx = sb("trx", [128, 128], BF16)
        tri = sb("tri", [128, 128], BF16)
        rst = sb("rst", [128, GB * 128], BF16)
        iot = sb("iot", [128, 512], BF16)
        on3 = sb("on3", [128, 128], BF16)
        m12 = sb("m12", [128, 128], BF16)
        wuv = sb("wuv", [128, 2 * H])
        wa = sb("wa", [128, H])
        wbt = sb("wbt", [128, 2, F])
        w2a = sb("w2a", [128, F])
        w2b = sb("w2b", [128, F])
        wwb = sb("wwb", [F + 1, F])
        bs = sb("bs", [3, 2, H])
        bp = sb("bp", [3, 3, H], BF16)
        be = sb("be", [3, 2, H])
        br = sb("br", [3, H], BF16)
        br2 = sb("br2", [3, GB, F], BF16)
        BD1 = sb("BD1", [128, 128])
        BD2 = sb("BD2", [128, 128])
        BI = sb("BI", [128, 3, 128])
        BH = sb("BH", [128, 3, 128])
        gb = sb("gb", [128, 7])
        gbs = sb("gbs", [128, 2])

        A8 = [sb(f"A8{i}", [128, GB, 128]) for i in range(2)]
        AT = [sb(f"AT{i}", [128, GB, 128]) for i in range(3)]
        X8 = [sb(f"X8{i}", [128, GB, F + 1]) for i in range(3)]
        XT = [sb(f"XT{i}", [128, PG, 128]) for i in range(2)]
        M8 = sb("M8", [128, GB, 128], BF16)
        RK = sb("RK", [128, GB, 128], BF16)
        Q8 = [sb(f"Q8{i}", [128, GB, 128], BF16) for i in range(2)]
        CM = sb("CM", [128, GB, NTH])
        NV = sb("NV", [128, GB], BF16)
        N12 = [sb(f"N12{i}", [128, GB], BF16) for i in range(2)]
        VO = sb("VO", [128, NB])
        VE = sb("VE", [128, NB])
        UA = [sb(f"UA{i}", [128, GB, H + 1]) for i in range(2)]
        VP = [sb(f"VP{i}", [128, 3, 2, H], BF16) for i in range(2)]
        E1 = sb("E1", [128, 2, H])
        SS = sb("SS", [128, 2, NROW], BF16)
        SE = sb("SE", [128, 2, NROW], BF16)
        OV = sb("OV", [128, 2, NROW], BF16)
        OVF = sb("OVF", [128, 2, NROW])
        GS = sb("GS", [128, 2 * NROW], BF16)
        OK = [sb(f"OK{i}", [128, C, 2 * NROW], BF16) for i in range(2)]
        OT = [sb(f"OT{i}", [128, 4, 128]) for i in range(2)]
        UV = [sb(f"UV{i}", [128, 4, H + 1]) for i in range(2)]
        RU = [sb(f"RU{i}", [128, 4, H]) for i in range(2)]
        NN = [sb(f"NN{i}", [128, 4]) for i in range(2)]
        TT = [sb(f"TT{i}", [128, C, H]) for i in range(2)]
        Z = [sb(f"Z{i}", [128, 4, H]) for i in range(2)]
        MT = [sb(f"MT{i}", [128, 2, 128]) for i in range(2)]
        MX = sb("MX", [F + 1, 2, 128])
        ST = sb("ST", [128, 512])
        XR = [sb(f"XR{i}", [128, GB, F]) for i in range(2)]
        X1 = sb("X1", [128, GB, F])
        SQ = sb("SQ", [128, GB, F])
        st = sb("st", [128, 4, GB])
        XG = sb("XG", [128, PG, 128])
        M1 = sb("M1", [128, PG, 128])
        M2 = sb("M2", [128, GB, F])
        MS = sb("MS", [128, PG, 128])
        GR = sb("GR", [128, 512])
        GZ = sb("GZ", [128, 512])
        GN = sb("GN", [128, 512])
        GT = sb("GT", [128, 512])
        fb = sb("fb", [128, 1], BF16)
        fi = sb("fi", [1, 1], I32)
        Y = sb("Y", [128, GB, F])
        YO = sb("YO", [128, GB, F])
        PS = ctx.enter_context(nc.psum_tensor("PS", [128, 8, 512], F32))

        freed = {}

        def bank(b, n=1):
            waits = [w for i in range(n) for w in freed.pop(b + i, [])]
            for i in range(n):
                assert (b + i) not in held
                held.add(b + i)
            return b, waits

        def free(b, tokens, n=1):
            for i in range(n):
                held.remove(b + i)
                freed[b + i] = list(tokens)

        held = set()

        def dma(dst, src, done, waits=()):
            return put("sync", lambda e: e.dma_start(dst, src), waits, done, 16)

        t_ms = put("gpsimd", lambda e: e.memset(BD1[:], 0.0), (), "ms")
        for t in (BD2[:], BI[:], BH[:], wbt[:]):
            t_ms = put("gpsimd", lambda e, t=t: e.memset(t, 0.0), (), "ms")
        t_ms = put("gpsimd", lambda e: e.memset(st[:, 3, :], -0.5), (), "ms")
        t_one = put("gpsimd", lambda e: e.memset(on3[:], 1.0), (), "ones")
        t_one = put("gpsimd", lambda e: e.memset(m12[:], -float(C)), (), "ones")
        for i in range(3):
            t_one = put("gpsimd", lambda e, i=i: e.memset(X8[i][:, :, F:F + 1], 1.0), (), "ones")

        t_c = dma(cs[:], cst, "dc")
        for h in range(2):
            dma(wa[64 * h:64 * h + 64, :], w1[0:F, :], "dw")
            dma(wuv[64 * h:64 * h + 64, H:2 * H], w1[F:2 * F, :], "dw")
            dma(w2b[64 * h:64 * h + 64, :], w2[128:H, :], "dw")
        dma(w2a[:], w2[0:128, :], "dw")
        dma(wwb[F:F + 1, :], b2.rearrange("(a n) -> a n", a=1), "dw")
        dma(bs[:, 0, :], b1.rearrange("(a n) -> a n", a=1).to_broadcast([3, H]), "dw")
        t_w = dma(bs[:, 1, 0:F], b2g.rearrange("(a n) -> a n", a=1).to_broadcast([3, F]), "dw")

        def load(g):
            T["A8", g] = dma(A8[g % 2][:], adj[:, g * GB:(g + 1) * GB, :], f"dA{g % 2}", [tk("mask", g - 2)])
            T["AT", g] = dma(AT[g % 3][:], adjt[:, g * GB:(g + 1) * GB, :], f"dT{g % 3}",
                             [tk("mt", PG * (g - 3) + PG - 1), tk("msg", g - 3)])
            T["X8", g] = dma(X8[g % 3][:, :, 0:F], x[:, g * GB:(g + 1) * GB, :], f"dX{g % 3}",
                             [t_one, tk("xr", PG * (g - 3) + PG - 1)])
            T["XT", g] = dma(XT[g % 2][:], xt[:, g * PG:(g + 1) * PG, :], f"dY{g % 2}",
                             [tk("uvp", PG * (g - 2) + PG - 1)])

        load(0)
        dma(wbt[:, 0, :], w1bt[0:128, :], "dg", [t_ms])
        dma(wbt[0:64, 1, :], w1bt[128:H, :], "dg")
        for h in range(2):
            s = slice(64 * h, 64 * h + 64)
            dma(BD1[s, s], w1g, "dg")
            dma(BD2[s, s], w2g, "dg")
            for k in range(3):
                dma(BI[s, k, s], wih[:, 64 * k:64 * k + 64], "dg")
                dma(BH[s, k, s], whh[:, 64 * k:64 * k + 64], "dg")
                dma(gb[s, k:k + 1], bih[64 * k:64 * k + 64].rearrange("(p a) -> p a", a=1), "dg")
                dma(gb[s, 3 + k:4 + k], bhh[64 * k:64 * k + 64].rearrange("(p a) -> p a", a=1), "dg")
            t_g = dma(gb[s, 6:7], b1g.rearrange("(p a) -> p a", a=1), "dg")
        load(1)

        for d, s in ((idb[:], CI), (trx[:], CTX), (tri[:], CTI)):
            put("vector", lambda e, d=d, s=s: e.tensor_copy(d, cs[:, s:s + 128]), [t_c], "cb")
        put("vector", lambda e: e.tensor_copy(rst[:], cs[:, CRS:CRS + GB * 128]), [], "cb")
        t_cb = put("vector", lambda e: e.tensor_copy(iot[:], cs[:, CIO:CIO + 512]), [], "cb")
        t_wu = put("vector", lambda e: e.tensor_tensor(wuv[:, 0:H], wa[:], wuv[:, H:2 * H], ALU.add), [t_w], "wu")

        w = [t_w]
        for i in range(3):
            src = bs if i == 0 else be
            for k, n in ((0, H), (1, F)):
                dst = bp[:, i, :] if k == 0 else br2[:, i, :]
                tb = put("vector", lambda e, dst=dst, src=src, k=k, n=n: e.tensor_copy(dst[:, 0:n], src[:, k, 0:n]), w, "bp")
            w = [tb]
            if i < 2:
                for k, n in ((0, H), (1, F)):
                    p = bp[:, i, :] if k == 0 else br2[:, i, :]
                    tb = put("vector", lambda e, p=p, src=src, k=k, n=n: e.tensor_tensor(
                        be[:, k, 0:n], src[:, k, 0:n], p[:, 0:n], ALU.subtract), w, "bp")
                w = [tb]
        for k, n, out_ in ((0, H, None), (1, F, None)):
            for i in range(3):
                p = bp[:, i, :] if k == 0 else br2[:, i, :]
                sel = cs[0:3, CSL + i:CSL + i + 1]
                o = be[:, k, 0:n]
                if i == 0:
                    tb = put("vector", lambda e, o=o, p=p, n=n, sel=sel: e.tensor_scalar(
                        o, p[:, 0:n], sel, None, ALU.mult), [t_c] + w, "bp")
                else:
                    tb = put("vector", lambda e, o=o, p=p, n=n, sel=sel: e.scalar_tensor_tensor(
                        o, p[:, 0:n], sel, o, ALU.mult, ALU.add), [tb], "bp")
        put("vector", lambda e: e.tensor_copy(br[:], be[:, 0, :]), [tb], "bp")
        t_b = put("vector", lambda e: e.tensor_copy(
            br2[:], be[:, 1, 0:F].unsqueeze(1).to_broadcast([3, GB, F])), [tb], "bp")
        t_gb = put("vector", lambda e: e.tensor_tensor(gbs[:], gb[:, 0:2], gb[:, 3:5], ALU.add), [t_g], "gbs")

        b, w = bank(6)

        def ww(e, b=b):
            e.matmul(PS[0:F, b, 0:F], wbt[:, 0, :], w2a[:], start=True, stop=False)
            return e.matmul(PS[0:F, b, 0:F], wbt[0:64, 1, :], w2b[0:64, :], start=False, stop=True)
        t_ww = put("tensor", ww, [t_g, t_w] + w, "ww")
        t_wb = put("vector", lambda e, b=b: e.tensor_scalar(wwb[0:F, :], PS[0:F, b, 0:F], -1.0, None, ALU.mult),
                   [t_ww], "wb")
        free(b, [t_wb])

        def ranks(g):
            i = g % 2
            T["mask", g] = put("vector", lambda e: e.tensor_scalar(M8[:], A8[i][:], 0.0, None, ALU.is_gt),
                               [T["A8", g]], "mask")
            yield
            T["rk", g] = put("vector", lambda e: e.tensor_tensor_scan(
                RK[:].rearrange("p b n -> p (b n)"), rst[:], M8[:].rearrange("p b n -> p (b n)"), 0.0, ALU.mult, ALU.add),
                [T["mask", g], t_cb], "rk")
            yield
            T["q8", g] = put("vector", lambda e: e.tensor_tensor(Q8[i][:], M8[:], RK[:], ALU.mult),
                             [T["rk", g], tk("gp", PG * (g - 2) + PG - 1)], "q8")
            a = put("vector", lambda e: e.tensor_tensor(
                CM[:], RK[:, :, 127:128].to_broadcast([128, GB, NTH]),
                cs[:, CTH:CTH + NTH].unsqueeze(1).to_broadcast([128, GB, NTH]), ALU.is_gt),
                [T["rk", g]], "cm")
            def red(e):
                with nc.allow_low_precision(reason="counts up to 11"):
                    return e.tensor_reduce(NV[:], CM[:], AX.X, ALU.add)
            a = put("vector", red, [a, tk("off", g - 1)], "nv")
            T["n12", g] = put("vector", lambda e: e.tensor_scalar(N12[i][:], NV[:], float(C), None, ALU.mult),
                              [a, tk("gp", PG * (g - 2) + PG - 1)], "n12")
            yield
            b, w = bank(6)

            def off(e, b=b):
                e.matmul(PS[:, b, 0:GB], trx[:], NV[:], start=True, stop=True)
                return e.matmul(PS[:, b, GB:2 * GB], tri[:], NV[:], start=True, stop=True)
            T["off", g] = put("tensor", off, [a] + w, "off")
            s = slice(g * GB, (g + 1) * GB)
            put("vector", lambda e: e.tensor_copy(VO[:, s], PS[:, b, 0:GB]), [T["off", g]], "vo")
            T["vo", g] = put("vector", lambda e: e.tensor_copy(VE[:, s], PS[:, b, GB:2 * GB]), [], "vo")
            T["c8", g] = put("vector", lambda e: e.scalar_tensor_tensor(
                UA[i][:, :, H], VO[:, s], float(C), RK[:, :, 127], ALU.mult, ALU.add),
                [T["vo", g], tk("uvv", PG * (g - 2) + PG - 1)], "c8")
            free(b, [T["vo", g]])

        def prep(p):
            g, j, i = p // PG, p % PG, p % 2
            gi = g % 2
            bq, w = bank(4, 2)

            def uvp(e, b=bq):
                for a in range(2):
                    s = slice(64 * a, 64 * a + 64)
                    e.matmul(PS[:, b + a, 0:2 * H], XT[gi][s, j, :], wuv[s, :], start=True, stop=False)
                    last = e.matmul(PS[:, b + a, 0:H], on3[0:3, :], br[:], start=False, stop=True)
                return last
            T["uvp", p] = put("tensor", uvp, [T["XT", g], t_wu, t_b, t_one] + w, "uvp")
            s2 = slice(2 * j, 2 * j + 2)
            for a in range(2):
                cc = 2 * p + a
                put("vector", lambda e, a=a, cc=cc: e.tensor_scalar(SS[:, a, :], iot[:, 0:NROW], VO[:, cc:cc + 1], None, ALU.is_ge),
                    [T["vo", g], t_cb], "ss")
                T["ss", p] = put("vector", lambda e, a=a, cc=cc: e.tensor_scalar(
                    SE[:, a, :], iot[:, 0:NROW], VE[:, cc:cc + 1], None, ALU.is_ge), [tk("gp", p - 1)], "ss")
            T["mt", p] = put("gpsimd", lambda e: e.tensor_scalar(MT[i][:], AT[g % 3][:, s2, :], 0.0, None, ALU.is_gt),
                             [T["AT", g], tk("mx", p - 2)], "mt")
            yield
            T["u", p] = put("scalar", lambda e, b=bq: e.activation(UA[gi][:, s2, 0:H], PS[:, b:b + 2, 0:H], ACT.Copy),
                            [T["uvp", p], tk("uvv", p - 8)], "u")
            T["v1", p] = put("scalar", lambda e, b=bq: e.activation(VP[i][:, 0, :, :], PS[:, b:b + 2, H:2 * H], ACT.Copy),
                             [tk("ga", p - 2)], "v1")
            T["ov", p] = put("vector", lambda e: e.tensor_tensor(OV[:], SS[:], SE[:], ALU.subtract),
                             [T["ss", p], tk("gp", p - 1), tk("ovf", p - 1), tk("ot", p - 1)], "ov")
            yield
            T["e1", p] = put("vector", lambda e, b=bq: e.tensor_tensor(E1[:], PS[:, b:b + 2, H:2 * H], VP[i][:, 0, :, :], ALU.subtract),
                             [T["v1", p], tk("v3", p - 1)], "e1")
            free(bq, [T["u", p], T["e1", p]], 2)
            T["ovf", p] = put("scalar", lambda e: e.activation(OVF[:], OV[:], ACT.Copy),
                              [T["ov", p], tk("uvv", p - 1)], "ovf")
            bg, w = bank(4)

            def gp(e, b=bg):
                o = PS[:, b, :]
                e.matmul(o, m12[0:1, :], iot[0:1, :], start=True, stop=False)
                for a in range(2):
                    oa = o[:, a * NROW:(a + 1) * NROW]
                    e.matmul(oa, Q8[gi][:, 2 * j + a, :], OV[:, a, :], start=False, stop=False)
                    last = e.matmul(oa, N12[gi][:, 2 * j + a:2 * j + a + 1].to_broadcast([128, 128]), SE[:, a, :],
                                    start=False, stop=(a == 1))
                return last
            T["gp", p] = put("tensor", gp, [T["q8", g], T["n12", g], T["ov", p]] + w, "gp")
            bt, w = bank(5)

            def ot(e, b=bt):
                o = PS[:, b, 0:256].bitcast(BF16)
                for k in range(4):
                    last = e.transpose(o[:, 128 * k:128 * k + 128], OV[:, k // 2, 128 * (k % 2):128 * (k % 2) + 128], idb[:])
                return last
            T["ot", p] = put("tensor", ot, w, "ot")
            yield
            T["v2", p] = put("scalar", lambda e: e.activation(VP[i][:, 1, :, :], E1[:], ACT.Copy), [T["e1", p]], "v2")
            T["gs", p] = put("scalar", lambda e, b=bg: e.activation(GS[:], PS[:, b, :], ACT.Copy),
                             [T["gp", p], tk("ok", p - 1)], "gs")
            free(bg, [T["gs", p]])
            yield
            T["v3", p] = put("gpsimd", lambda e: e.tensor_tensor(VP[i][:, 2, :, :], E1[:], VP[i][:, 1, :, :], ALU.subtract),
                             [T["v2", p]], "v3")
            T["otc", p] = put("scalar", lambda e, b=bt: e.activation(
                OT[i][:].rearrange("p k n -> p (k n)"), PS[:, b, 0:256].bitcast(BF16), ACT.Copy), [T["ot", p], tk("stp", p - 2)], "otc")
            free(bt, [T["otc", p]])
            bu, w = bank(4, 2)

            def uvv(e, b=bu):
                for k in range(4):
                    last = e.matmul(PS[:, b + k // 2, 256 * (k % 2):256 * (k % 2) + H + 1],
                                    OVF[:, k // 2, 128 * (k % 2):128 * (k % 2) + 128], UA[gi][:, 2 * j + k // 2, :],
                                    start=True, stop=True)
                return last
            T["uvv", p] = put("tensor", uvv, [T["ovf", p], T["u", p], T["c8", g]] + w, "uvv")
            yield
            pu = PS[:, bu:bu + 2, :].rearrange("p b (k n) -> p (b k) n", k=2)
            T["uv", p] = put("scalar", lambda e: e.activation(UV[i][:], pu[:, :, 0:H + 1], ACT.Copy),
                             [T["uvv", p], tk("max", p - 2), tk("nn", p - 2)], "uv")
            T["ru", p] = put("scalar", lambda e: e.activation(RU[i][:], pu[:, :, 0:H], ACT.Relu), [tk("z", p - 2)], "ru")
            free(bu, [T["ru", p]], 2)
            for r in range(C):
                T["ok", p] = put("vector", lambda e, r=r: e.tensor_scalar(OK[i][:, r, :], GS[:], float(r + 1), None, ALU.is_equal),
                                 [T["gs", p], tk("ga", p - 2)], "ok")
                if r % 3 == 2:
                    yield
            a = put("vector", lambda e: e.tensor_tensor(NN[i][:], UV[i][:, :, H], cs[:, CKV:CKV + 4], ALU.subtract),
                    [T["uv", p], tk("z", p - 2)], "nn0")
            T["nn", p] = put("vector", lambda e: e.tensor_scalar(NN[i][:], NN[i][:], 0.0, None, ALU.min), [a], "nn")

        count = [0]

        def quad(p, k, r):
            i, m = p % 2, count[0]
            count[0] += 1
            a, vt = k // 2, k % 2

            def gather(e):
                for s in range(4):
                    o = PS[:, 2 * (m % 2) + s // 2, 256 * (s % 2):256 * (s % 2) + H]
                    lhs = OK[i][:, 4 * r + s, a * NROW + vt * 128:a * NROW + vt * 128 + 128]
                    for c in range(3):
                        last = e.matmul(o, lhs, VP[i][:, c, a, :], start=(c == 0), stop=(c == 2))
                return last
            T["ga", p] = ga = put("tensor", gather, [T["ok", p], T["v1", p], T["v2", p], T["v3", p], tk("mx4", m - 2)], "ga")
            src = PS[:, 2 * (m % 2):2 * (m % 2) + 2, :].rearrange("p b (s n) -> p (b s) n", s=2)[:, :, 0:H]
            t = TT[k % 2]
            T["max", p] = T["mx4", m] = put("vector", lambda e: e.tensor_tensor(
                t[:, 4 * r:4 * r + 4, :], src, UV[i][:, k:k + 1, 0:H].to_broadcast([128, 4, H]), ALU.max),
                [ga, T["uv", p], tk("tz", 4 * p + k - 2)], "max")
            if r:
                T["add", 4 * p + k] = put("gpsimd", lambda e: e.tensor_tensor(
                    t[:, 0:4, :], t[:, 0:4, :], t[:, 4 * r:4 * r + 4, :], ALU.add),
                    [T["mx4", m], tk("add", 4 * p + k)], "add")

        def close(p, k):
            i, t = p % 2, TT[k % 2]
            a = put("vector", lambda e: e.tensor_tensor(t[:, 0:2, :], t[:, 0:2, :], t[:, 2:4, :], ALU.add),
                    [T["add", 4 * p + k]], "t2")
            a = put("vector", lambda e: e.tensor_tensor(t[:, 0, :], t[:, 0, :], t[:, 1, :], ALU.add), [a], "t2")
            T["z", p] = T["tz", 4 * p + k] = put("vector", lambda e: e.scalar_tensor_tensor(
                Z[i][:, k, :], RU[i][:, k, :], NN[i][:, k:k + 1], t[:, 0, :], ALU.mult, ALU.add),
                [a, T["ru", p], T["nn", p], tk("stp", p - 2)], "z")

        def tail(p, dense=False):
            g, j, i = p // PG, p % PG, p % 2
            bm, w = bank(6)

            def mx(e, b=bm):
                for a in range(2):
                    last = e.matmul(PS[0:F + 1, b, 128 * a:128 * a + 128], X8[g % 3][:, 2 * j + a, :], MT[i][:, a, :],
                                    start=True, stop=True)
                return last
            T["mx", p] = put("tensor", mx, [T["X8", g], T["mt", p], t_one] + w, "mx")
            yield
            T["mxc", p] = put("scalar", lambda e, b=bm: e.activation(
                MX[:].rearrange("p a n -> p (a n)"), PS[0:F + 1, b, 0:256], ACT.Copy), [T["mx", p], tk("o0", p - 1)], "mxc")
            free(bm, [T["mxc", p]])
            yield
            b1_, w = bank(6)

            def stp(e, b=b1_):
                for a in range(2):
                    for h in range(2):
                        o = PS[0:128 - 64 * h, b, 256 * h + 128 * a:256 * h + 128 * a + 128]
                        if dense:
                            last = e.matmul(o, Z[i][:, 2 * a, 128 * h:128 + 64 * h], cs[:, CI:CI + 128], start=True, stop=True)
                            continue
                        for vt in range(2):
                            zz = Z[i][:, 2 * a + vt, 0:128] if h == 0 else Z[i][:, 2 * a + vt, 128:H]
                            last = e.matmul(o, zz, OT[i][:, 2 * a + vt, :], start=(vt == 0), stop=(vt == 1))
                return last
            T["stp", p] = put("tensor", stp, [T["z", p], tk("otc", p)] + w, "stp")
            yield
            put("scalar", lambda e, b=b1_: e.activation(ST[:, 0:256], PS[:, b, 0:256], ACT.Copy),
                [T["stp", p], tk("o0", p - 1)], "stc")
            T["stc", p] = put("scalar", lambda e, b=b1_: e.activation(ST[0:64, 256:512], PS[0:64, b, 256:512], ACT.Copy),
                              [], "stc")
            free(b1_, [T["stc", p]])
            yield
            b2_, w = bank(6)

            def o0(e, b=b2_):
                for a in range(2):
                    o = PS[:, b, 64 * a:64 * a + 64]
                    e.matmul(o, ST[:, 128 * a:128 * a + 128], w2a[:], start=True, stop=False)
                    e.matmul(o, ST[0:64, 256 + 128 * a:384 + 128 * a], w2b[0:64, :], start=False, stop=False)
                    last = e.matmul(o, MX[:, a, :], wwb[:], start=False, stop=True)
                return last
            T["o0", p] = put("tensor", o0, [T["stc", p], T["mxc", p], t_wb] + w, "o0")
            yield
            T["xr", p] = put("vector", lambda e, b=b2_: e.tensor_tensor(
                XR[g % 2][:, 2 * j:2 * j + 2, :], PS[:, b, 0:128].rearrange("p (a n) -> p a n", a=2),
                X8[g % 3][:, 2 * j:2 * j + 2, 0:F], ALU.add), [T["o0", p], tk("lna", g - 2)], "xr")
            free(b2_, [T["xr", p]])

        def norm(src, dst, waits, done):
            a = put("vector", lambda e: e.tensor_reduce(st[:, 0, :], src, AX.X, ALU.add), waits, "ln")
            a = put("vector", lambda e: e.scalar_tensor_tensor(
                dst, st[:, 0, :].unsqueeze(2).to_broadcast([128, GB, F]), -1.0 / F, src, ALU.mult, ALU.add), [a], "ln")
            read = a
            yield read
            a = put("gpsimd", lambda e: e.tensor_tensor(SQ[:], dst, dst, ALU.mult), [a], "sq")
            yield read
            a = put("vector", lambda e: e.tensor_reduce(st[:, 1, :], SQ[:], AX.X, ALU.add), [a], "ln")
            a = put("vector", lambda e: e.tensor_scalar(st[:, 2, :], st[:, 1, :], F * EPS, None, ALU.add), [a], "ln")
            a = put("gpsimd", lambda e: e.tensor_tensor(st[:, 2, :], st[:, 2, :], st[:, 3, :], ALU.pow), [a, t_ms], "pow")
            yield read
            T[done] = put("vector", lambda e: e.scalar_tensor_tensor(
                dst, dst, F ** 0.5, st[:, 2, :].unsqueeze(2).to_broadcast([128, GB, F]), ALU.mult, ALU.mult), [a], "ln")

        def layer1(g, where=None):
            for a in norm(XR[g % 2][:], X1[:], [T["xr", PG * g + PG - 1], tk("y", g - 1)], ("x1", g)):
                T["lna", g] = a
                yield
            yield
            b, w = bank(7)

            def xg(e, b=b):
                for k in range(PG):
                    last = e.transpose(PS[:, b, 128 * k:128 * k + 128],
                                       X1[:, 2 * k:2 * k + 2, :].rearrange("p a n -> p (a n)"), cs[:, CI:CI + 128])
                return last
            a = put("tensor", xg, [T["x1", g], t_c] + w, "xg")
            yield
            XGf = XG[:].rearrange("p k n -> p (k n)")
            T["xgc", g] = put("scalar", lambda e, b=b: e.activation(XGf, PS[:, b, :], ACT.Copy),
                              [a, tk("h", g - 1)], "xgc")
            free(b, [T["xgc", g]])
            yield
            b, w = bank(7)
            a = put("tensor", lambda e, b=b: e.matmul(PS[:, b, :], BD1[:], XGf, start=True, stop=True),
                    [T["xgc", g], t_g] + w, "m1")
            yield
            a = put("scalar", lambda e, b=b: e.activation(M1[:].rearrange("p k n -> p (k n)"), PS[:, b, :], ACT.Relu,
                                                          bias=gb[:, 6:7]), [a, t_g], "m1c")
            free(b, [a])
            yield
            b, w = bank(7)

            def m2(e, b=b):
                e.matmul(PS[:, b, :], on3[0:3, :], br2[:].rearrange("p b n -> p (b n)"), start=True, stop=False)
                for k in range(PG):
                    last = e.matmul(PS[:, b, 128 * k:128 * k + 128], M1[:, k, :], BD2[:], start=False, stop=(k == PG - 1))
                return last
            a = put("tensor", m2, [a] + w, "m2")
            yield
            a = put("scalar", lambda e, b=b: e.activation(M2[:].rearrange("p b n -> p (b n)"), PS[:, b, :], ACT.Relu),
                    [a], "m2c")
            free(b, [a])
            yield
            b, w = bank(7)

            def msg(e, b=b):
                for k in range(GB):
                    s = slice(64 * (k % 2), 64 * (k % 2) + 64)
                    last = e.matmul(PS[s, b, 128 * (k // 2):128 * (k // 2) + 128], M2[:, k, :], AT[g % 3][:, k, :],
                                    start=True, stop=True)
                return last
            T["msg", g] = put("tensor", msg, [a, T["AT", g]] + w, "msg")
            yield
            MSf = MS[:].rearrange("p k n -> p (k n)")
            t_m = put("scalar", lambda e, b=b: e.activation(MSf, PS[:, b, :], ACT.Relu), [T["msg", g]], "msc")
            free(b, [t_m])
            yield
            for k, dst in ((0, GR), (1, GZ)):
                b, w = bank(7)

                def gate(e, b=b, k=k):
                    e.matmul(PS[:, b, :], BH[:, k, :], XGf, start=True, stop=False)
                    return e.matmul(PS[:, b, :], BI[:, k, :], MSf, start=False, stop=True)
                a = put("tensor", gate, [t_m] + w, "gate")
                yield
                a = put("scalar", lambda e, b=b, dst=dst, k=k: e.activation(dst[:], PS[:, b, :], ACT.Sigmoid,
                                                                            bias=gbs[:, k:k + 1]), [a, t_gb], "sig")
                free(b, [a])
                if k == 0:
                    t_r = a
                else:
                    t_z = a
            b, w = bank(7)
            a = put("tensor", lambda e, b=b: e.matmul(PS[:, b, :], BH[:, 2, :], XGf, start=True, stop=True), w, "gate")
            yield
            t = put("vector", lambda e, b=b: e.scalar_tensor_tensor(GT[:], PS[:, b, :], gb[:, 5:6], GR[:], ALU.add, ALU.mult),
                    [a, t_r, t_g], "gt")
            free(b, [t])
            b, w = bank(7)
            a = put("tensor", lambda e, b=b: e.matmul(PS[:, b, :], BI[:, 2, :], MSf, start=True, stop=True), w, "gate")
            yield
            t = put("vector", lambda e, b=b: e.tensor_tensor(GT[:], PS[:, b, :], GT[:], ALU.add), [a, t], "gt")
            free(b, [t])
            yield
            t = put("scalar", lambda e: e.activation(GN[:], GT[:], ACT.Tanh, bias=gb[:, 2:3]), [t], "tanh")
            yield
            t = put("gpsimd", lambda e: e.tensor_tensor(GT[:], XGf, GN[:], ALU.subtract), [t], "gd")
            t = put("gpsimd", lambda e: e.tensor_tensor(GT[:], GT[:], GZ[:], ALU.mult), [t, t_z], "gd")
            yield
            t = T["h", g] = put("gpsimd", lambda e: e.tensor_tensor(GT[:], GT[:], GN[:], ALU.add), [t], "h")
            yield
            b, w = bank(7)

            def yt(e, b=b):
                for k in range(PG):
                    last = e.transpose(PS[:, b, 128 * k:128 * k + 128], GT[:, 128 * k:128 * k + 128], cs[:, CI:CI + 128])
                return last
            a = put("tensor", yt, [t] + w, "yt")
            yield
            T["y", g] = put("vector", lambda e, b=b: e.tensor_tensor(
                Y[:].rearrange("p b n -> p (b n)"), PS[:, b, :], X1[:].rearrange("p b n -> p (b n)"), ALU.add), [a], "y")
            free(b, [T["y", g]])
            yield
            for _ in norm(Y[:], YO[:], [T["y", g], tk("out", g - 1)], ("yo", g)):
                yield
            where = slice(g * GB, (g + 1) * GB) if where is None else where
            T["out", g] = dma(out[:, where, :], YO[:], "out", [T["yo", g]])

        def finish(gen):
            for _ in gen:
                pass

        finish(ranks(0))
        finish(prep(0))
        chains = []
        clock = 0
        for p in range(NP):
            g, j = p // PG, p % PG
            nxt = prep(p + 1) if p + 1 < NP else iter(())
            prv = tail(p - 1) if p else iter(())
            if j == 0 and g + 1 < NG:
                rk = ranks(g + 1)
            if j == 0 and g and g + 1 < NG:
                load(g + 1)
            for k in range(4):
                for r in range(3):
                    quad(p, k, r)
                    if k and r == 0:
                        close(p, k - 1)
                    next(prv, 0)
                    next(nxt, 0)
                    if j == 1 and g + 1 < NG:
                        next(rk, 0)
                    clock += 1
                    if clock % 3:
                        for c in chains:
                            next(c, 0)
            close(p, 3)
            finish(prv)
            finish(nxt)
            if j == 0 and g:
                chains.append(layer1(g - 1))
            if j == 3:
                for c in chains:
                    finish(c)
                chains.clear()
        finish(tail(NP - 1))
        finish(layer1(NG - 1))

        a = put("vector", lambda e: e.tensor_reduce(st[:, 0, 0:1], VE[:], AX.X, ALU.max),
                [T["vo", NG - 1], T["yo", NG - 1]], "flag")
        a = put("vector", lambda e: e.tensor_scalar(fb[:], st[:, 0, 0:1], float(LIMIT), None, ALU.is_gt), [a], "flag")
        b, w = bank(6)
        a = put("tensor", lambda e: e.matmul(PS[0:1, 6, 0:1], fb[:], on3[:, 0:1], start=True, stop=True), [a] + w, "fsum")
        a = put("vector", lambda e: e.tensor_copy(fi[:], PS[0:1, 6, 0:1]), [a], "flag")
        free(6, [a])

        def emit(q):
            with nc.Block() as block:
                @block.tensor
                def _(e):
                    q.run("tensor", e)

                @block.vector
                def _(e):
                    q.run("vector", e)

                @block.scalar
                def _(e):
                    q.run("scalar", e)

                @block.gpsimd
                def _(e):
                    q.run("gpsimd", e)

                @block.sync
                def _(e):
                    q.run("sync", e)
                    e.wait_ge(q.sems["out"], q.value["out"])
                    if "flag" in q.sems:
                        e.wait_ge(q.sems["flag"], q.value["flag"])

        emit(q)

        over = nc.values_load(fi[:], min_val=0, max_val=128)
        with nc.If(over > 0):
            with nc.Fori(0, NG) as gv:
                q = Queues(lambda name: ctx.enter_context(nc.semaphore("g_" + name)))
                T.clear()
                freed.clear()
                t_one = t_wu = t_b = t_wb = t_c = t_g = t_gb = t_ms = None
                here = bass.ds(gv * GB, GB)
                T["A8", 0] = dma(A8[0][:], adj[:, here, :], "dA")
                T["AT", 0] = dma(AT[0][:], adjt[:, here, :], "dT")
                T["X8", 0] = dma(X8[0][:, :, 0:F], x[:, here, :], "dX")
                T["XT", 0] = dma(XT[0][:], xt[:, bass.ds(gv * PG, PG), :], "dY")
                t_mk = put("vector", lambda e: e.tensor_scalar(A8[0][:], A8[0][:], 0.0, None, ALU.is_gt), [T["A8", 0]], "mask")
                m = 0
                t_z = None
                for p in range(PG):
                    i = p % 2

                    def uvd(e, p=p):
                        for a in range(2):
                            s = slice(64 * a, 64 * a + 64)
                            e.matmul(PS[:, 4 + a, 0:2 * H], XT[0][s, p, :], wuv[s, :], start=True, stop=False)
                            last = e.matmul(PS[:, 4 + a, 0:H], on3[0:3, :], br[:], start=False, stop=True)
                        return last
                    a = put("tensor", uvd, [T["XT", 0], tk("u", p - 1)], "uvp")
                    put("scalar", lambda e: e.activation(UV[0][:, 0:2, 0:H], PS[:, 4:6, 0:H], ACT.Copy), [a, tk("z", p - 1)], "u")
                    T["u", p] = put("scalar", lambda e: e.activation(E1[:], PS[:, 4:6, H:2 * H], ACT.Copy), [tk("ga", p - 1)], "u")
                    T["mt", p] = put("gpsimd", lambda e, i=i, p=p: e.tensor_scalar(
                        MT[i][:], AT[0][:, 2 * p:2 * p + 2, :], 0.0, None, ALU.is_gt), [T["AT", 0], tk("mx", p - 2)], "mt")
                    for a in range(2):
                        for r in range(32):
                            def spread(e, a=a, r=r, m=m):
                                for s in range(4):
                                    k = 4 * r + s
                                    last = e.matmul(PS[:, 2 * (m % 2) + s // 2, 256 * (s % 2):256 * (s % 2) + H],
                                                    cs[:, CI + k:CI + k + 1].to_broadcast([128, 128]), E1[:, a, :],
                                                    start=True, stop=True)
                                return last
                            T["ga", p] = ga = put("tensor", spread, [T["u", p], tk("mx4", m - 2)], "ga")
                            src = PS[:, 2 * (m % 2):2 * (m % 2) + 2, :].rearrange("p b (s n) -> p (b s) n", s=2)[:, :, 0:H]
                            t = TT[0][:, 0:4, :]
                            w = T["mx4", m] = put("vector", lambda e, t=t, src=src, a=a: e.tensor_tensor(
                                t, src, UV[0][:, a:a + 1, 0:H].to_broadcast([128, 4, H]), ALU.max), [ga, T["u", p], t_z], "max")
                            w = put("vector", lambda e, t=t, a=a, p=p, r=r: e.tensor_tensor(
                                t, t, A8[0][:, 2 * p + a, 4 * r:4 * r + 4].unsqueeze(2).to_broadcast([128, 4, H]), ALU.mult),
                                [w, t_mk], "md")
                            dst = Z[i][:, 2 * a, :] if r == 0 else TT[0][:, 4, :]
                            w = put("vector", lambda e, t=t, dst=dst: e.tensor_reduce(
                                dst, t.rearrange("p s n -> p n s"), AX.X, ALU.add), [w, tk("stp", p - 2)], "rd")
                            if r:
                                w = put("vector", lambda e, i=i, a=a: e.tensor_tensor(
                                    Z[i][:, 2 * a, :], Z[i][:, 2 * a, :], TT[0][:, 4, :], ALU.add), [w], "z")
                            T["z", p] = t_z = w
                            m += 1
                    finish(tail(p, dense=True))
                finish(layer1(0, here))
                emit(q)
                for s in q.sems.values():
                    nc.gpsimd.sem_clear(s)
                nc.all_engine_barrier()


def kernel(x, adj, L0_gnn_W1, L0_gnn_b1, L0_gnn_W2, L0_gnn_b2, L1_gnn_W1, L1_gnn_b1, L1_gnn_W2, L1_gnn_b2,
           L1_gnn_W_ih, L1_gnn_b_ih, L1_gnn_W_hh, L1_gnn_b_hh):
    import concourse.bacc as _bacc
    from concourse.bass_utils import run_bass_kernel_spmd as _run

    x, adj = np.asarray(x), np.asarray(adj)
    w1 = np.asarray(L0_gnn_W1)
    arrays = {
        "adj": adj.transpose(1, 0, 2),
        "adjt": adj.transpose(2, 0, 1),
        "x": x.transpose(1, 0, 2),
        "xt": x.reshape(NP, 2, N, F).transpose(1, 3, 0, 2).reshape(2 * F, NP, N),
        "w1": w1,
        "w1bt": w1[F:].T,
        "b1": L0_gnn_b1,
        "w2": L0_gnn_W2,
        "b2": L0_gnn_b2,
        "w1g": L1_gnn_W1,
        "b1g": L1_gnn_b1,
        "w2g": L1_gnn_W2,
        "b2g": L1_gnn_b2,
        "wih": np.asarray(L1_gnn_W_ih).T,
        "bih": L1_gnn_b_ih,
        "whh": np.asarray(L1_gnn_W_hh).T,
        "bhh": L1_gnn_b_hh,
        "cst": constants(),
    }
    nc = _bacc.Bacc("TRN2", target_bir_lowering=False, num_devices=1)
    feeds, args = {}, []
    for name, a in arrays.items():
        a = np.ascontiguousarray(a)
        feeds[f"in_{name}"] = a
        args.append(nc.dram_tensor(f"in_{name}", a.shape, mybir.dt.from_np(a.dtype), kind="ExternalInput").ap())
    out = nc.dram_tensor("out_0", (N, NB, F), F32, kind="ExternalOutput").ap()
    build(nc, *args, out)
    r = _run(nc, [feeds], core_ids=[0])
    return np.ascontiguousarray(r.results[0]["out_0"].transpose(1, 0, 2))
```

```python
from contextlib import ExitStack

import numpy as np

import concourse.bass as bass
from concourse import mybir

F32 = mybir.dt.float32
BF16 = mybir.dt.bfloat16
I32 = mybir.dt.int32
ALU = mybir.AluOpType
ACT = mybir.ActivationFunctionType
AX = mybir.AxisListType

NB = 128
N = 128
F = 64
H = 192
GB = 8
NG = NB // GB
PG = GB // 2
NP = NB // 2
C0 = 13
C1 = 8
NTH = -(-(N - C0) // C1)
LIMIT = 128
EPS = 1e-5

CI = 0
CTX = CI + 128
CTI = CTX + 128
CRS = CTI + 128
CIO = CRS + GB * 128
CTH = CIO + 128
CSL = CTH + NTH
CML = CSL + 3
CMR = CML + 128
CC0 = CMR + 256
CC1 = CC0 + 64
NC = CC1 + 64


def constants():
    c = np.zeros((128, NC), np.float32)
    i = np.arange(128)
    c[:, CI:CI + 128] = np.eye(128)
    c[:, CTX:CTX + 128] = i[:, None] < i[None, :]
    c[:, CTI:CTI + 128] = i[:, None] <= i[None, :]
    c[:, CRS:CRS + GB * 128] = (np.arange(GB * 128) % 128 != 0)[None, :]
    c[:, CIO:CIO + 128] = i[None, :]
    c[:, CTH:CTH + NTH] = (C0 + C1 * np.arange(NTH))[None, :]
    c[:, CSL:CSL + 3] = i[:, None] == np.arange(3)[None, :]
    c[0, CML:CML + 128] = -C1
    c[1, CML:CML + 128] = -C0
    c[0, CMR:CMR + 256] = np.arange(256) % 128
    c[1, CMR:CMR + 256] = 1
    c[0:64, CC0:CC0 + 64] = np.eye(64) - 1 / 64
    c[64:128, CC1:CC1 + 64] = np.eye(64) - 1 / 64
    return c


class Queues:

    def __init__(self, sem):
        self.sem = sem
        self.sems = {}
        self.value = {}
        self.lists = {e: [] for e in ("tensor", "vector", "scalar", "gpsimd", "sync")}

    def put(self, engine, make, waits=(), done=None, n=1):
        token = None
        if done:
            if done not in self.sems:
                self.sems[done] = self.sem(done)
                self.value[done] = 0
            self.value[done] += n
            token = (done, self.value[done])
        self.lists[engine].append((make, [w for w in waits if w], done, n))
        return token

    def run(self, name, engine):
        seen = {}
        for make, waits, done, n in self.lists[name]:
            need = {}
            for s, v in waits:
                if v > seen.get(s, 0):
                    need[s] = max(need.get(s, 0), v)
            for s, v in need.items():
                engine.wait_ge(self.sems[s], v)
                seen[s] = v
            last = make(engine)
            if done:
                last.then_inc(self.sems[done], n)


def build(nc, adj, adjt, xt, w1, w1bt, b1, w2, b2, w1g, b1g, w2g, b2g, wih, bih, whh, bhh, cst, out):
    ctx = ExitStack()
    with ctx:
        def sb(name, shape, dt=F32):
            return ctx.enter_context(nc.sbuf_tensor(name, shape, dt))

        q = Queues(lambda name: ctx.enter_context(nc.semaphore(name)))
        T = {}

        def put(*args, **kw):
            return q.put(*args, **kw)

        def tk(name, i):
            return T.get((name, i))

        cs = sb("cs", [128, NC])
        idb = sb("idb", [128, 128], BF16)
        trx = sb("trx", [128, 128], BF16)
        tri = sb("tri", [128, 128], BF16)
        rst = sb("rst", [128, GB * 128], BF16)
        iot = sb("iot", [128, 128], BF16)
        mlr = sb("mlr", [2, 384], BF16)
        on3 = sb("on3", [128, 128], BF16)
        wuv = sb("wuv", [128, 2 * H + F])
        wa = sb("wa", [128, H])
        wbt = sb("wbt", [128, 2, F])
        w2r = sb("w2r", [128, 2, F])
        w2c = sb("w2c", [128, 2, F])
        b2r = sb("b2r", [3, F])
        wst = sb("wst", [128, 6])
        bs = sb("bs", [3, 2, H + F])
        bp = sb("bp", [3, 2, 3, H + F], BF16)
        be = sb("be", [3, 2, H + F])
        br = sb("br", [3, H + F], BF16)
        br2 = sb("br2", [3, GB, F], BF16)
        BD1 = sb("BD1", [128, 128])
        BD2 = sb("BD2", [128, 128])
        BDC = sb("BDC", [128, 128])
        BI = sb("BI", [128, 3, 128])
        BH = sb("BH", [128, 3, 128])
        gb = sb("gb", [128, 7])
        gbs = sb("gbs", [128, 2])

        A8 = [sb(f"A8{i}", [128, GB, 128]) for i in range(2)]
        AT = [sb(f"AT{i}", [128, GB, 128]) for i in range(3)]
        XT = [sb(f"XT{i}", [128, PG, 128]) for i in range(3)]
        M8 = sb("M8", [128, GB, 128], BF16)
        RK = sb("RK", [128, GB, 128], BF16)
        Q8 = [sb(f"Q8{i}", [128, GB, 128], BF16) for i in range(2)]
        CM = sb("CM", [128, GB, NTH])
        NV = sb("NV", [128, GB], BF16)
        N12 = [sb(f"N12{i}", [128, GB], BF16) for i in range(2)]
        VO = sb("VO", [128, NB])
        VE = sb("VE", [128, NB])
        NN = sb("NN", [128, NB])
        UA = [sb(f"UA{i}", [128, 2, H + F]) for i in range(3)]
        RU = [sb(f"RU{i}", [128, 2, H]) for i in range(2)]
        VP = [sb(f"VP{i}", [128, 3, 2, H], BF16) for i in range(2)]
        E1 = sb("E1", [128, 2, H])
        SS = sb("SS", [128, 2, 128], BF16)
        SE = sb("SE", [128, 2, 128], BF16)
        OV = sb("OV", [128, 2, 128], BF16)
        OVF = sb("OVF", [128, 2, 128])
        GS = sb("GS", [128, 512], BF16)
        OK = [sb(f"OK{i}", [128, C1, 512], BF16) for i in range(2)]
        OK0 = [sb(f"OKX{i}", [128, C0 - C1, 256], BF16) for i in range(2)]
        OT = [sb(f"OT{i}", [128, 2, 128]) for i in range(2)]
        UV = [sb(f"UV{i}", [128, 2, H]) for i in range(2)]
        TA = [[sb(f"TA{i}{t}", [128, 2, 2, H]) for t in range(2)] for i in range(2)]
        TR = [sb(f"TR{i}", [128, 2, 2, H]) for i in range(4)]
        TS = [sb(f"TS{i}", [128, 2, H]) for i in range(2)]
        S = [sb(f"S{i}", [128, 2, H]) for i in range(2)]
        Z = sb("Z", [128, 2, H])
        MT = [sb(f"MT{i}", [128, 2, 128]) for i in range(3)]
        ST = sb("ST", [128, 512])
        XR = [sb(f"XR{i}", [128, GB, F]) for i in range(2)]
        X1 = sb("X1", [128, GB, F])
        SQ = sb("SQ", [128, GB, F])
        st = sb("st", [128, 4, GB])
        XG = sb("XG", [128, PG, 128])
        M1 = sb("M1", [128, PG, 128])
        M2 = sb("M2", [128, GB, F])
        MS = sb("MS", [128, PG, 128])
        GR = sb("GR", [128, 512])
        GZ = sb("GZ", [128, 512])
        GN = sb("GN", [128, 512])
        GT = sb("GT", [128, 512])
        fb = sb("fb", [128, 1], BF16)
        fi = sb("fi", [1, 1], I32)
        Y = sb("Y", [128, GB, F])
        YO = sb("YO", [128, GB, F])
        PS = ctx.enter_context(nc.psum_tensor("PS", [128, 8, 512], F32))

        freed = {}

        def bank(b, n=1):
            waits = [w for i in range(n) for w in freed.pop(b + i, [])]
            for i in range(n):
                assert (b + i) not in held
                held.add(b + i)
            return b, waits

        def free(b, tokens, n=1):
            for i in range(n):
                held.remove(b + i)
                freed[b + i] = list(tokens)

        held = set()

        def dma(dst, src, done, waits=()):
            return put("sync", lambda e: e.dma_start(dst, src), waits, done, 16)

        for t in (BD1[:], BD2[:], BI[:], BH[:], wbt[:], w2r[:], bs[:]):
            t_ms = put("gpsimd", lambda e, t=t: e.memset(t, 0.0), (), "ms")
        t_ms = put("gpsimd", lambda e: e.memset(st[:, 3, :], -0.5), (), "ms")
        t_one = put("gpsimd", lambda e: e.memset(on3[:], 1.0), (), "ones")

        t_c = dma(cs[:], cst, "dc")
        for h in range(2):
            dma(wa[64 * h:64 * h + 64, :], w1[0:F, :], "dw")
            dma(wuv[64 * h:64 * h + 64, H + F:2 * H + F], w1[F:2 * F, :], "dw")
        dma(w2r[:, 0, :], w2[0:128, :], "dw", [t_ms])
        dma(w2r[0:64, 1, :], w2[128:H, :], "dw")
        dma(wbt[:, 0, :], w1bt[0:128, :], "dw")
        dma(wbt[0:64, 1, :], w1bt[128:H, :], "dw")
        dma(b2r[:], b2.rearrange("(a n) -> a n", a=1).to_broadcast([3, F]), "dw")
        dma(bs[:, 0, 0:H], b1.rearrange("(a n) -> a n", a=1).to_broadcast([3, H]), "dw")
        t_w = dma(bs[:, 1, 0:F], b2g.rearrange("(a n) -> a n", a=1).to_broadcast([3, F]), "dw")

        def load(g):
            T["A8", g] = dma(A8[g % 2][:], adj[:, g * GB:(g + 1) * GB, :], f"dA{g % 2}", [tk("mask", g - 2)])
            T["XT", g] = dma(XT[g % 3][:], xt[:, g * PG:(g + 1) * PG, :], f"dY{g % 3}",
                             [tk("o0", PG * (g - 3) + PG - 1)])
            T["AT", g] = dma(AT[g % 3][:], adjt[:, g * GB:(g + 1) * GB, :], f"dT{g % 3}",
                             [tk("mt", PG * (g - 3) + PG - 1), tk("msg", g - 3)])

        load(0)
        for h in range(2):
            s = slice(64 * h, 64 * h + 64)
            dma(BD1[s, s], w1g, "dg")
            dma(BD2[s, s], w2g, "dg")
            for k in range(3):
                dma(BI[s, k, s], wih[:, 64 * k:64 * k + 64], "dg")
                dma(BH[s, k, s], whh[:, 64 * k:64 * k + 64], "dg")
                dma(gb[s, k:k + 1], bih[64 * k:64 * k + 64].rearrange("(p a) -> p a", a=1), "dg")
                dma(gb[s, 3 + k:4 + k], bhh[64 * k:64 * k + 64].rearrange("(p a) -> p a", a=1), "dg")
            t_g = dma(gb[s, 6:7], b1g.rearrange("(p a) -> p a", a=1), "dg")
        load(1)

        for d, s in ((idb[:], CI), (trx[:], CTX), (tri[:], CTI), (iot[:], CIO)):
            put("vector", lambda e, d=d, s=s: e.tensor_copy(d, cs[:, s:s + 128]), [t_c], "cb")
        put("vector", lambda e: e.tensor_copy(rst[:], cs[:, CRS:CRS + GB * 128]), [], "cb")
        put("vector", lambda e: e.tensor_copy(mlr[:], cs[0:2, CML:CML + 384]), [], "cb")
        put("vector", lambda e: e.tensor_copy(BDC[:, 0:64], cs[:, CC0:CC0 + 64]), [], "cb")
        t_cb = put("vector", lambda e: e.tensor_copy(BDC[:, 64:128], cs[:, CC1:CC1 + 64]), [], "cb")
        t_wu = put("vector", lambda e: e.tensor_tensor(wuv[:, 0:H], wa[:], wuv[:, H + F:2 * H + F], ALU.add), [t_w], "wu")

        t = put("vector", lambda e: e.tensor_reduce(wst[:, 0:2], w2r[:], AX.X, ALU.add), [t_w], "wc")
        t = put("vector", lambda e: e.scalar_tensor_tensor(
            w2c[:], wst[:, 0:2].unsqueeze(2).to_broadcast([128, 2, F]), -1.0 / F, w2r[:], ALU.mult, ALU.add), [t], "wc")
        t_w2 = t
        t = put("vector", lambda e: e.tensor_reduce(wst[0:3, 2:3], b2r[:], AX.X, ALU.add), [], "wc")
        t = put("vector", lambda e: e.scalar_tensor_tensor(
            bs[:, 0, H:H + F], wst[0:3, 2:3].to_broadcast([3, F]), -1.0 / F, b2r[:], ALU.mult, ALU.add), [t, t_ms], "wc")

        w = [t]
        for i in range(3):
            src = bs if i == 0 else be
            t = put("vector", lambda e, i=i, src=src: e.tensor_copy(bp[:, :, i, :], src[:]), w, "bp")
            if i < 2:
                t = put("vector", lambda e, i=i, src=src: e.tensor_tensor(be[:], src[:], bp[:, :, i, :], ALU.subtract),
                        [t], "bp")
            w = [t]
        for i in range(3):
            sel = cs[0:3, CSL + i:CSL + i + 1]
            if i == 0:
                t = put("vector", lambda e, i=i, sel=sel: e.tensor_scalar(be[:], bp[:, :, i, :], sel, None, ALU.mult),
                        [t_c] + w, "bp")
            else:
                t = put("vector", lambda e, i=i, sel=sel: e.scalar_tensor_tensor(
                    be[:], bp[:, :, i, :], sel, be[:], ALU.mult, ALU.add), [t], "bp")
        put("vector", lambda e: e.tensor_copy(br[:], be[:, 0, :]), [t], "bp")
        t_b = put("vector", lambda e: e.tensor_copy(
            br2[:], be[:, 1, 0:F].unsqueeze(1).to_broadcast([3, GB, F])), [], "bp")
        t_gb = put("vector", lambda e: e.tensor_tensor(gbs[:], gb[:, 0:2], gb[:, 3:5], ALU.add), [t_g], "gbs")

        b, w = bank(6)

        def ww(e, b=b):
            for h in range(2):
                s = slice(64 * h, 64 * h + 64)
                e.matmul(PS[s, b, 0:F], wbt[:, 0, :], w2c[:, 0, :], start=True, stop=False)
                last = e.matmul(PS[s, b, 0:F], wbt[:, 1, :], w2c[:, 1, :], start=False, stop=True)
            return last
        t_ww = put("tensor", ww, [t_w, t_w2] + w, "ww")
        t_wb = put("vector", lambda e, b=b: e.tensor_scalar(wuv[:, H:H + F], PS[:, b, 0:F], -1.0, None, ALU.mult),
                   [t_ww], "wb")
        free(b, [t_wb])

        def ranks(g):
            i = g % 2
            T["mask", g] = put("vector", lambda e: e.tensor_scalar(M8[:], A8[i][:], 0.0, None, ALU.is_gt),
                               [T["A8", g], tk("q8", g - 1)], "mask")
            yield
            T["rk", g] = put("vector", lambda e: e.tensor_tensor_scan(
                RK[:].rearrange("p b n -> p (b n)"), rst[:], M8[:].rearrange("p b n -> p (b n)"), 0.0, ALU.mult, ALU.add),
                [T["mask", g], t_cb, tk("nn", g - 1)], "rk")
            yield
            T["q8", g] = put("vector", lambda e: e.tensor_tensor(Q8[i][:], M8[:], RK[:], ALU.mult),
                             [T["rk", g], tk("gp", PG * (g - 2) + PG - 1)], "q8")
            a = put("vector", lambda e: e.tensor_tensor(
                CM[:], RK[:, :, 127:128].to_broadcast([128, GB, NTH]),
                cs[:, CTH:CTH + NTH].unsqueeze(1).to_broadcast([128, GB, NTH]), ALU.is_gt),
                [T["rk", g]], "cm")

            def red(e):
                with nc.allow_low_precision(reason="counts up to 15"):
                    return e.tensor_reduce(NV[:], CM[:], AX.X, ALU.add)
            a = put("vector", red, [a, tk("off", g - 1)], "nv")
            yield
            T["n12", g] = put("vector", lambda e: e.tensor_scalar(N12[i][:], NV[:], float(C1), None, ALU.mult),
                              [a, tk("gp", PG * (g - 2) + PG - 1)], "n12")
            b, w = bank(6)

            def off(e, b=b):
                e.matmul(PS[:, b, 0:GB], trx[:], NV[:], start=True, stop=True)
                return e.matmul(PS[:, b, GB:2 * GB], tri[:], NV[:], start=True, stop=True)
            T["off", g] = put("tensor", off, [a] + w, "off")
            s = slice(g * GB, (g + 1) * GB)
            t = put("vector", lambda e: e.scalar_tensor_tensor(
                NN[:, s], NV[:], -float(C1), RK[:, :, 127], ALU.mult, ALU.add), [], "nn")
            T["nn", g] = put("vector", lambda e: e.tensor_scalar(NN[:, s], NN[:, s], -float(C0), None, ALU.add), [t], "nn")
            put("vector", lambda e: e.tensor_copy(VO[:, s], PS[:, b, 0:GB]), [T["off", g]], "vo")
            T["vo", g] = put("vector", lambda e: e.tensor_copy(VE[:, s], PS[:, b, GB:2 * GB]), [], "vo")
            free(b, [T["vo", g]])

        def products(e, x, p):
            for a in range(2):
                s = slice(64 * a, 64 * a + 64)
                e.matmul(PS[:, 4 + a, 0:2 * H + F], x[s, p % PG, :], wuv[s, :], start=True, stop=False)
            for a in range(2):
                last = e.matmul(PS[:, 4 + a, 0:H + F], on3[0:3, :], br[:], start=False, stop=True)
            return last

        def prep(p):
            g, j, i = p // PG, p % PG, p % 2
            gi = g % 2
            b, w = bank(4, 2)
            T["uvp", p] = put("tensor", lambda e: products(e, XT[g % 3], p), [T["XT", g], t_wu, t_wb, t_b, t_one] + w, "uvp")
            s2 = slice(2 * j, 2 * j + 2)
            for a in range(2):
                cc = 2 * p + a
                put("vector", lambda e, a=a, cc=cc: e.tensor_scalar(SS[:, a, :], iot[:], VO[:, cc:cc + 1], None, ALU.is_ge),
                    [T["vo", g], t_cb, tk("ov", p - 1)], "ss")
                T["ss", p] = put("vector", lambda e, a=a, cc=cc: e.tensor_scalar(
                    SE[:, a, :], iot[:], VE[:, cc:cc + 1], None, ALU.is_ge), [tk("gp", p - 1)], "ss")
            T["mt", p] = put("gpsimd", lambda e: e.tensor_scalar(MT[p % 3][:], AT[g % 3][:, s2, :], 0.0, None, ALU.is_gt),
                             [T["AT", g], tk("o0", p - 3)], "mt")
            yield
            T["v1", p] = put("scalar", lambda e: e.activation(VP[i][:, 0, :, :], PS[:, 4:6, H + F:2 * H + F], ACT.Copy),
                             [T["uvp", p], tk("ga", p - 2)], "v1")
            T["ov", p] = put("vector", lambda e: e.tensor_tensor(OV[:], SS[:], SE[:], ALU.subtract),
                             [T["ss", p], tk("gp", p - 1), tk("ovf", p - 1), tk("ot", p - 1)], "ov")
            T["u", p] = put("scalar", lambda e: e.activation(UA[p % 3][:], PS[:, 4:6, 0:H + F], ACT.Copy),
                            [tk("mx0", p - 3), tk("o0", p - 3)], "u")
            T["ru", p] = put("scalar", lambda e: e.activation(RU[i][:], PS[:, 4:6, 0:H], ACT.Relu), [tk("s0", p - 2)], "ru")
            yield
            T["e1", p] = put("vector", lambda e: e.tensor_tensor(E1[:], PS[:, 4:6, H + F:2 * H + F], VP[i][:, 0, :, :], ALU.subtract),
                             [T["ru", p], tk("v3", p - 1)], "e1")
            T["ovf", p] = put("scalar", lambda e: e.activation(OVF[:], OV[:], ACT.Copy),
                              [T["ov", p], tk("uvv", p - 1)], "ovf")
            free(4, [T["e1", p]], 2)
            yield
            T["v2", p] = put("scalar", lambda e: e.activation(VP[i][:, 1, :, :], E1[:], ACT.Copy), [T["e1", p]], "v2")
            _, wg = bank(4)
            _, wt = bank(5)

            def gp(e):
                o = PS[:, 4, 0:256]
                e.matmul(o, mlr[0:2, 0:128], mlr[0:2, 128:384], start=True, stop=False)
                for a in range(2):
                    oa = PS[:, 4, 128 * a:128 * a + 128]
                    e.matmul(oa, Q8[gi][:, 2 * j + a, :], OV[:, a, :], start=False, stop=False)
                    last = e.matmul(oa, N12[gi][:, 2 * j + a:2 * j + a + 1].to_broadcast([128, 128]), SE[:, a, :],
                                    start=False, stop=(a == 1))
                return last
            T["gp", p] = put("tensor", gp, [T["q8", g], T["n12", g], T["ov", p]] + wg, "gp")
            pt = PS[:, 5, 0:256].bitcast(BF16)

            def ot(e):
                for a in range(2):
                    e.transpose(pt[:, 128 * a:128 * a + 128], Q8[gi][:, 2 * j + a, :], idb[:])
                for a in range(2):
                    last = e.transpose(pt[:, 256 + 128 * a:384 + 128 * a], OV[:, a, :], idb[:])
                return last
            T["ot", p] = T["gp", p] = put("tensor", ot, wt, "ot")
            yield
            T["v3", p] = put("gpsimd", lambda e: e.tensor_tensor(VP[i][:, 2, :, :], E1[:], VP[i][:, 1, :, :], ALU.subtract),
                             [T["v2", p]], "v3")
            put("scalar", lambda e: e.activation(GS[:, 0:256], pt[:, 0:256], ACT.Copy), [T["ot", p], tk("ok", p - 1)], "gs")
            T["gs", p] = put("scalar", lambda e: e.activation(GS[:, 256:512], PS[:, 4, 0:256], ACT.Copy), [], "gs")
            free(4, [T["gs", p]])
            T["otc", p] = put("scalar", lambda e: e.activation(
                OT[i][:].rearrange("p k n -> p (k n)"), pt[:, 256:512], ACT.Copy), [tk("seg", p - 2)], "otc")
            free(5, [T["otc", p]])
            yield
            _, w = bank(4)

            def uvv(e):
                for a in range(2):
                    last = e.matmul(PS[:, 4, 256 * a:256 * a + H], OVF[:, a, :], UA[p % 3][:, a, 0:H], start=True, stop=True)
                return last
            T["uvv", p] = put("tensor", uvv, [T["ovf", p], T["u", p]] + w, "uvv")
            for r in range(C1):
                T["ok", p] = put("vector", lambda e, r=r: e.tensor_scalar(OK[i][:, r, :], GS[:], float(r + 1), None, ALU.is_equal),
                                 [T["gs", p], tk("ga", p - 2)], "ok")
                if r % 4 == 3:
                    yield
            T["uv", p] = put("scalar", lambda e: e.activation(
                UV[i][:], PS[:, 4, :].rearrange("p (k n) -> p k n", k=2)[:, :, 0:H], ACT.Copy),
                [T["uvv", p], tk("mx1", p - 2)], "uv")
            free(4, [T["uv", p]])
            for r in range(C1, C0):
                T["ok", p] = put("vector", lambda e, r=r: e.tensor_scalar(
                    OK0[i][:, r - C1, :], GS[:, 0:256], float(r + 1), None, ALU.is_equal), [], "ok")

        count = [0]

        def quad(p, t, r, n):
            i, m = p % 2, count[0]
            count[0] += 1

            def gather(e):
                for a in range(2):
                    for s in range(n):
                        k = 256 * t + 128 * a
                        lhs = OK[i][:, r + s, k:k + 128] if r + s < C1 else OK0[i][:, r + s - C1, k:k + 128]
                        o = PS[:, 2 * (m % 2) + a, 256 * s:256 * s + H]
                        for c in range(3):
                            last = e.matmul(o, lhs, VP[i][:, c, a, :], start=(c == 0), stop=(c == 2))
                return last
            T["ga", p] = ga = put("tensor", gather, [T["ok", p], T["v1", p], T["v2", p], T["v3", p], tk("m", m - 2)], "ga")
            src = PS[:, 2 * (m % 2):2 * (m % 2) + 2, :].rearrange("p b (s n) -> p b s n", s=2)[:, :, 0:n, 0:H]
            u = (UV[i] if t else UA[p % 3])[:, :, 0:H].unsqueeze(2).to_broadcast([128, 2, n, H])
            if n == 1:
                dst, w = TS[i][:].unsqueeze(2), tk("s0", p - 2)
            elif r == 0:
                dst, w = TA[i][t][:], tk(f"close{t}", p - 2)
            else:
                ring[0] += 1
                k = ring[0]
                dst, w = TR[k % 4][:], tk("add", k - 4)
            T[f"mx{t}", p] = T["m", m] = mx = put("vector", lambda e: e.tensor_tensor(dst, src, u, ALU.max),
                                                  [ga, T["uv" if t else "u", p], w], "max")
            if n == 2 and r:
                T["acc", t, p] = T["add", k] = put("gpsimd", lambda e: e.tensor_tensor(
                    TA[i][t][:], TA[i][t][:], dst, ALU.add), [mx, T.get(("acc", t, p))], "add")

        ring = [0]

        def own(p):
            i, g = p % 2, p // PG
            t = put("vector", lambda e: e.tensor_tensor(S[i][:], TA[i][0][:, :, 0, :], TA[i][0][:, :, 1, :], ALU.add),
                    [T["acc", 0, p], tk("st", p - 2)], "s0")
            T["close0", p] = t
            yield
            t = put("vector", lambda e: e.tensor_tensor(S[i][:], S[i][:], TS[i][:], ALU.add), [t, T["mx0", p]], "s0")
            for a in range(2):
                T["s0", p] = put("vector", lambda e, a=a: e.scalar_tensor_tensor(
                    S[i][:, a, :], RU[i][:, a, :], NN[:, 2 * p + a:2 * p + a + 1], S[i][:, a, :], ALU.mult, ALU.add),
                    [t, T["ru", p], T["nn", g]], "s0")

        def tail(p, dense=False):
            g, j, i = p // PG, p % PG, p % 2
            if not dense:
                yield
                T["close1", p] = t = put("vector", lambda e: e.tensor_tensor(
                    Z[:], TA[i][1][:, :, 0, :], TA[i][1][:, :, 1, :], ALU.add), [T["acc", 1, p], tk("seg", p - 1)], "z")
                yield
                b, w = bank(6)

                def seg(e):
                    for a in range(2):
                        last = e.matmul(PS[:, 6, 256 * a:256 * a + H], OT[i][:, a, :], Z[:, a, :], start=True, stop=True)
                    return last
                T["seg", p] = t = put("tensor", seg, [t, T["otc", p]] + w, "seg")
                yield
                T["s", p] = put("vector", lambda e: e.tensor_tensor(
                    S[i][:], S[i][:], PS[:, 6, :].rearrange("p (k n) -> p k n", k=2)[:, :, 0:H], ALU.add),
                    [t, T["s0", p]], "s")
                free(6, [T["s", p]])
                yield
            b, w = bank(6)

            def stp(e):
                for a in range(2):
                    e.transpose(PS[:, 6, 128 * a:128 * a + 128], S[i][:, a, 0:128], cs[:, CI:CI + 128])
                    last = e.transpose(PS[0:64, 6, 256 + 128 * a:384 + 128 * a], S[i][:, a, 128:H], cs[:, CI:CI + 128])
                return last
            T["st", p] = put("tensor", stp, [T["s", p], t_c] + w, "st")
            yield
            put("scalar", lambda e: e.activation(ST[:, 0:256], PS[:, 6, 0:256], ACT.Copy), [T["st", p], tk("o0", p - 1)], "stc")
            T["stc", p] = put("scalar", lambda e: e.activation(ST[0:64, 256:512], PS[0:64, 6, 256:512], ACT.Copy), [], "stc")
            free(6, [T["stc", p]])
            yield
            b, w = bank(6)

            def o0(e):
                for a in range(2):
                    o = PS[:, 6, 64 * a:64 * a + 64]
                    e.matmul(o, XT[g % 3][:, j, :], BDC[:, 64 * a:64 * a + 64], start=True, stop=False)
                    e.matmul(o, MT[p % 3][:, a, :], UA[p % 3][:, a, H:H + F], start=False, stop=False)
                    e.matmul(o, ST[:, 128 * a:128 * a + 128], w2c[:, 0, :], start=False, stop=False)
                    last = e.matmul(o, ST[0:64, 256 + 128 * a:384 + 128 * a], w2c[0:64, 1, :], start=False, stop=True)
                return last
            T["o0", p] = put("tensor", o0, [T["stc", p], T["mt", p], T["u", p], t_w2, t_cb] + w, "o0")
            yield
            T["xr", p] = put("scalar", lambda e: e.activation(
                XR[g % 2][:, 2 * j:2 * j + 2, :].rearrange("p a n -> p (a n)"), PS[:, 6, 0:128], ACT.Copy),
                [T["o0", p], tk("x1", g - 2)], "xr")
            free(6, [T["xr", p]])

        def norm(src, dst, waits, done):
            a = put("scalar", lambda e: e.activation(SQ[:], src, ACT.Square), waits + [T.get("sq")], "sq")
            yield
            T["sq"] = a = put("vector", lambda e: e.tensor_reduce(st[:, 1, :], SQ[:], AX.X, ALU.add), [a, T.get("rs")], "ln")
            a = put("vector", lambda e: e.tensor_scalar(st[:, 2, :], st[:, 1, :], F * EPS, None, ALU.add), [a], "ln")
            a = put("gpsimd", lambda e: e.tensor_tensor(st[:, 2, :], st[:, 2, :], st[:, 3, :], ALU.pow), [a, t_ms], "pow")
            yield
            yield
            T[done] = T["rs"] = put("vector", lambda e: e.scalar_tensor_tensor(
                dst, src, F ** 0.5, st[:, 2, :].unsqueeze(2).to_broadcast([128, GB, F]), ALU.mult, ALU.mult), [a], "ln")

        def layer1(g, where=None):
            for _ in norm(XR[g % 2][:], X1[:], [T["xr", PG * g + PG - 1], tk("y", g - 1)], ("x1", g)):
                yield
            yield
            b, w = bank(7)

            def xg(e, b=b):
                for k in range(PG):
                    last = e.transpose(PS[:, b, 128 * k:128 * k + 128],
                                       X1[:, 2 * k:2 * k + 2, :].rearrange("p a n -> p (a n)"), cs[:, CI:CI + 128])
                return last
            a = put("tensor", xg, [T["x1", g], t_c] + w, "xg")
            yield
            XGf = XG[:].rearrange("p k n -> p (k n)")
            T["xgc", g] = put("scalar", lambda e, b=b: e.activation(XGf, PS[:, b, :], ACT.Copy),
                              [a, tk("h", g - 1)], "xgc")
            free(b, [T["xgc", g]])
            yield
            b, w = bank(7)
            a = put("tensor", lambda e, b=b: e.matmul(PS[:, b, :], BD1[:], XGf, start=True, stop=True),
                    [T["xgc", g], t_g] + w, "m1")
            yield
            a = put("scalar", lambda e, b=b: e.activation(M1[:].rearrange("p k n -> p (k n)"), PS[:, b, :], ACT.Relu,
                                                          bias=gb[:, 6:7]), [a, t_g], "m1c")
            free(b, [a])
            yield
            b, w = bank(7)

            def m2(e, b=b):
                e.matmul(PS[:, b, :], on3[0:3, :], br2[:].rearrange("p b n -> p (b n)"), start=True, stop=False)
                for k in range(PG):
                    last = e.matmul(PS[:, b, 128 * k:128 * k + 128], M1[:, k, :], BD2[:], start=False, stop=(k == PG - 1))
                return last
            a = put("tensor", m2, [a] + w, "m2")
            yield
            a = put("scalar", lambda e, b=b: e.activation(M2[:].rearrange("p b n -> p (b n)"), PS[:, b, :], ACT.Relu),
                    [a], "m2c")
            free(b, [a])
            yield
            b, w = bank(7)

            def msg(e, b=b):
                for k in range(GB):
                    s = slice(64 * (k % 2), 64 * (k % 2) + 64)
                    last = e.matmul(PS[s, b, 128 * (k // 2):128 * (k // 2) + 128], M2[:, k, :], AT[g % 3][:, k, :],
                                    start=True, stop=True)
                return last
            T["msg", g] = put("tensor", msg, [a, T["AT", g]] + w, "msg")
            yield
            MSf = MS[:].rearrange("p k n -> p (k n)")
            t_m = put("scalar", lambda e, b=b: e.activation(MSf, PS[:, b, :], ACT.Relu), [T["msg", g]], "msc")
            free(b, [t_m])
            yield
            for k, dst in ((0, GR), (1, GZ)):
                b, w = bank(7)

                def gate(e, b=b, k=k):
                    e.matmul(PS[:, b, :], BH[:, k, :], XGf, start=True, stop=False)
                    return e.matmul(PS[:, b, :], BI[:, k, :], MSf, start=False, stop=True)
                a = put("tensor", gate, [t_m] + w, "gate")
                yield
                a = put("scalar", lambda e, b=b, dst=dst, k=k: e.activation(dst[:], PS[:, b, :], ACT.Sigmoid,
                                                                            bias=gbs[:, k:k + 1]), [a, t_gb], "sig")
                free(b, [a])
                if k == 0:
                    t_r = a
                else:
                    t_z = a
            b, w = bank(7)
            a = put("tensor", lambda e, b=b: e.matmul(PS[:, b, :], BH[:, 2, :], XGf, start=True, stop=True), w, "gate")
            yield
            t = put("vector", lambda e, b=b: e.scalar_tensor_tensor(GT[:], PS[:, b, :], gb[:, 5:6], GR[:], ALU.add, ALU.mult),
                    [a, t_r, t_g], "gt")
            free(b, [t])
            b, w = bank(7)
            a = put("tensor", lambda e, b=b: e.matmul(PS[:, b, :], BI[:, 2, :], MSf, start=True, stop=True), w, "gate")
            yield
            t = put("vector", lambda e, b=b: e.tensor_tensor(GT[:], PS[:, b, :], GT[:], ALU.add), [a, t], "gt")
            free(b, [t])
            yield
            t = put("scalar", lambda e: e.activation(GN[:], GT[:], ACT.Tanh, bias=gb[:, 2:3]), [t], "tanh")
            yield
            t = put("gpsimd", lambda e: e.tensor_tensor(GT[:], XGf, GN[:], ALU.subtract), [t], "gd")
            t = put("gpsimd", lambda e: e.tensor_tensor(GT[:], GT[:], GZ[:], ALU.mult), [t, t_z], "gd")
            yield
            t = T["h", g] = put("gpsimd", lambda e: e.tensor_tensor(GT[:], GT[:], GN[:], ALU.add), [t], "h")
            yield
            b, w = bank(7)

            def yt(e, b=b):
                for k in range(PG):
                    last = e.matmul(PS[:, b, 128 * k:128 * k + 128], GT[:, 128 * k:128 * k + 128], BDC[:],
                                    start=True, stop=True)
                return last
            a = put("tensor", yt, [t] + w, "yt")
            yield
            T["y", g] = put("vector", lambda e, b=b: e.tensor_tensor(
                Y[:].rearrange("p b n -> p (b n)"), PS[:, b, :], X1[:].rearrange("p b n -> p (b n)"), ALU.add), [a], "y")
            free(b, [T["y", g]])
            yield
            for _ in norm(Y[:], YO[:], [T["y", g], tk("out", g - 1)], ("yo", g)):
                yield
            where = slice(g * GB, (g + 1) * GB) if where is None else where
            T["out", g] = dma(out[:, where, :], YO[:], "out", [T["yo", g]])

        def finish(gen):
            for _ in gen:
                pass

        finish(ranks(0))
        finish(prep(0))
        parts = [(0, r, min(2, C0 - r)) for r in range(0, C0, 2)] + [(1, r, 2) for r in range(0, C1, 2)]
        deep = iter(())
        clock = 0
        for p in range(NP):
            g, j = p // PG, p % PG
            nxt = prep(p + 1) if p + 1 < NP else iter(())
            prv = tail(p - 1) if p else iter(())
            if j == 0 and g and g + 1 < NG:
                load(g + 1)
            if j == 0:
                rk = ranks(g + 1) if g + 1 < NG else iter(())
            for n, (t, r, k) in enumerate(parts):
                quad(p, t, r, k)
                next(prv, 0)
                next(nxt, 0)
                if j == 1:
                    next(rk, 0)
                if t and r == 2:
                    mine = own(p)
                if t and r >= 2:
                    next(mine, 0)
                clock += 1
                if j and (clock % 4):
                    next(deep, 0)
            finish(mine)
            finish(prv)
            finish(nxt)
            if j == 1:
                finish(rk)
            if j == 0 and g:
                deep = layer1(g - 1)
            if j == 3:
                finish(deep)
        finish(tail(NP - 1))
        finish(layer1(NG - 1))

        a = put("vector", lambda e: e.tensor_reduce(st[:, 0, 0:1], VE[:], AX.X, ALU.max),
                [T["vo", NG - 1], T["yo", NG - 1]], "flag")
        a = put("vector", lambda e: e.tensor_scalar(fb[:], st[:, 0, 0:1], float(LIMIT), None, ALU.is_gt), [a], "flag")
        _, w = bank(6)
        a = put("tensor", lambda e: e.matmul(PS[0:1, 6, 0:1], fb[:], on3[:, 0:1], start=True, stop=True), [a] + w, "fsum")
        a = put("vector", lambda e: e.tensor_copy(fi[:], PS[0:1, 6, 0:1]), [a], "flag")
        free(6, [a])

        def emit(q):
            with nc.Block() as block:
                @block.tensor
                def _(e):
                    q.run("tensor", e)

                @block.vector
                def _(e):
                    q.run("vector", e)

                @block.scalar
                def _(e):
                    q.run("scalar", e)

                @block.gpsimd
                def _(e):
                    q.run("gpsimd", e)

                @block.sync
                def _(e):
                    q.run("sync", e)
                    e.wait_ge(q.sems["out"], q.value["out"])
                    if "flag" in q.sems:
                        e.wait_ge(q.sems["flag"], q.value["flag"])

        emit(q)

        over = nc.values_load(fi[:], min_val=0, max_val=128)
        with nc.If(over > 0):
            with nc.Fori(0, NG) as gv:
                q = Queues(lambda name: ctx.enter_context(nc.semaphore("g_" + name)))
                T.clear()
                freed.clear()
                t_one = t_wu = t_b = t_wb = t_c = t_g = t_gb = t_ms = t_w2 = t_cb = None
                here = bass.ds(gv * GB, GB)
                T["A8", 0] = dma(A8[0][:], adj[:, here, :], "dA")
                T["AT", 0] = dma(AT[0][:], adjt[:, here, :], "dT")
                T["XT", 0] = dma(XT[0][:], xt[:, bass.ds(gv * PG, PG), :], "dY")
                t_mk = put("vector", lambda e: e.tensor_scalar(A8[0][:], A8[0][:], 0.0, None, ALU.is_gt), [T["A8", 0]], "mask")
                m = 0
                t_z = None
                for p in range(PG):
                    i = p % 2
                    a = put("tensor", lambda e, p=p: products(e, XT[0], p), [T["XT", 0], tk("u", p - 1)], "uvp")
                    put("scalar", lambda e, p=p: e.activation(UA[p % 3][:], PS[:, 4:6, 0:H + F], ACT.Copy),
                        [a, tk("s", p - 3), tk("o0", p - 3)], "u")
                    T["u", p] = put("scalar", lambda e: e.activation(E1[:], PS[:, 4:6, H + F:2 * H + F], ACT.Copy),
                                    [tk("ga", p - 1)], "u")
                    T["mt", p] = put("gpsimd", lambda e, p=p: e.tensor_scalar(
                        MT[p % 3][:], AT[0][:, 2 * p:2 * p + 2, :], 0.0, None, ALU.is_gt), [T["AT", 0], tk("o0", p - 3)], "mt")
                    for a in range(2):
                        for r in range(32):
                            def spread(e, a=a, r=r, m=m):
                                for s in range(4):
                                    k = 4 * r + s
                                    last = e.matmul(PS[:, 2 * (m % 2) + s // 2, 256 * (s % 2):256 * (s % 2) + H],
                                                    cs[:, CI + k:CI + k + 1].to_broadcast([128, 128]), E1[:, a, :],
                                                    start=True, stop=True)
                                return last
                            T["ga", p] = ga = put("tensor", spread, [T["u", p], tk("m", m - 2)], "ga")
                            src = PS[:, 2 * (m % 2):2 * (m % 2) + 2, :].rearrange("p b (s n) -> p (b s) n", s=2)[:, :, 0:H]
                            t = TR[0][:].rearrange("p a s n -> p (a s) n")
                            w = T["m", m] = put("vector", lambda e, t=t, src=src, a=a, p=p: e.tensor_tensor(
                                t, src, UA[p % 3][:, a:a + 1, 0:H].to_broadcast([128, 4, H]), ALU.max), [ga, T["u", p], t_z], "max")
                            w = put("vector", lambda e, t=t, a=a, p=p, r=r: e.tensor_tensor(
                                t, t, A8[0][:, 2 * p + a, 4 * r:4 * r + 4].unsqueeze(2).to_broadcast([128, 4, H]), ALU.mult),
                                [w, t_mk], "md")
                            dst = S[i][:, a, :] if r == 0 else TS[0][:, 0, :]
                            w = put("vector", lambda e, t=t, dst=dst: e.tensor_reduce(
                                dst, t.rearrange("p s n -> p n s"), AX.X, ALU.add), [w, tk("st", p - 2)], "rd")
                            if r:
                                w = put("vector", lambda e, i=i, a=a: e.tensor_tensor(
                                    S[i][:, a, :], S[i][:, a, :], TS[0][:, 0, :], ALU.add), [w], "z")
                            T["s", p] = t_z = w
                            m += 1
                    finish(tail(p, dense=True))
                finish(layer1(0, here))
                emit(q)
                for s in q.sems.values():
                    nc.gpsimd.sem_clear(s)
                nc.all_engine_barrier()


def kernel(x, adj, L0_gnn_W1, L0_gnn_b1, L0_gnn_W2, L0_gnn_b2, L1_gnn_W1, L1_gnn_b1, L1_gnn_W2, L1_gnn_b2,
           L1_gnn_W_ih, L1_gnn_b_ih, L1_gnn_W_hh, L1_gnn_b_hh):
    import concourse.bacc as _bacc
    from concourse.bass_utils import run_bass_kernel_spmd as _run

    x, adj = np.asarray(x), np.asarray(adj)
    w1 = np.asarray(L0_gnn_W1)
    arrays = {
        "adj": adj.transpose(1, 0, 2),
        "adjt": adj.transpose(2, 0, 1),
        "xt": x.reshape(NP, 2, N, F).transpose(1, 3, 0, 2).reshape(2 * F, NP, N),
        "w1": w1,
        "w1bt": w1[F:].T,
        "b1": L0_gnn_b1,
        "w2": L0_gnn_W2,
        "b2": L0_gnn_b2,
        "w1g": L1_gnn_W1,
        "b1g": L1_gnn_b1,
        "w2g": L1_gnn_W2,
        "b2g": L1_gnn_b2,
        "wih": np.asarray(L1_gnn_W_ih).T,
        "bih": L1_gnn_b_ih,
        "whh": np.asarray(L1_gnn_W_hh).T,
        "bhh": L1_gnn_b_hh,
        "cst": constants(),
    }
    nc = _bacc.Bacc("TRN2", target_bir_lowering=False, num_devices=1)
    feeds, args = {}, []
    for name, a in arrays.items():
        a = np.ascontiguousarray(a)
        feeds[f"in_{name}"] = a
        args.append(nc.dram_tensor(f"in_{name}", a.shape, mybir.dt.from_np(a.dtype), kind="ExternalInput").ap())
    out = nc.dram_tensor("out_0", (N, NB, F), F32, kind="ExternalOutput").ap()
    build(nc, *args, out)
    r = _run(nc, [feeds], core_ids=[0])
    return np.ascontiguousarray(r.results[0]["out_0"].transpose(1, 0, 2))
```

```python
from contextlib import ExitStack

import numpy as np

import concourse.bass as bass
from concourse import mybir

F32 = mybir.dt.float32
BF16 = mybir.dt.bfloat16
F16 = mybir.dt.float16
I32 = mybir.dt.int32
ALU = mybir.AluOpType
ACT = mybir.ActivationFunctionType
AX = mybir.AxisListType

NB = 128
N = 128
F = 64
H = 192
GB = 8
NG = NB // GB
PG = GB // 2
NP = NB // 2
C0 = 13
C1 = 8
NTH = -(-(N - C0) // C1)
LIMIT = 128
EPS = 1e-5
SCALE = 256.0
MOST, LEAST = 3.6e9, 24.0

RT = 5

ORDER = (
    ("drppd", "r", "tprt", "rp", "d", "td", "p", "", "pppprp", "pppo", "ttod"),
    ("poptptdp", "", "d", "td", "pp", "tpdpp", "pp", "p", "odtp", "od", "pd"),
    ("pop", "tptp", "", "p", "t", "p", "", "pppppdp", "op", "dtto", "poddd"),
    ("tpppp", "ddt", "", "", "pt", "pppptppd", "p", "ootpdopdpd", "pppp", "pppp", "dd"),
)

CI = 0
CTX = CI + 128
CTI = CTX + 128
CRS = CTI + 128
CIO = CRS + GB * 128
CTH = CIO + 128
CSL = CTH + NTH
CML = CSL + 3
CMR = CML + 128
CC0 = CMR + 256
CC1 = CC0 + 64
NC = CC1 + 64


def constants():
    c = np.zeros((128, NC), np.float32)
    i = np.arange(128)
    c[:, CI:CI + 128] = np.eye(128)
    c[:, CTX:CTX + 128] = i[:, None] < i[None, :]
    c[:, CTI:CTI + 128] = i[:, None] <= i[None, :]
    c[:, CRS:CRS + GB * 128] = (np.arange(GB * 128) % 128 != 0)[None, :]
    c[:, CIO:CIO + 128] = i[None, :]
    c[:, CTH:CTH + NTH] = (C0 + C1 * np.arange(NTH))[None, :]
    c[:, CSL:CSL + 3] = i[:, None] == np.arange(3)[None, :]
    c[0, CML:CML + 128] = -C1
    c[1, CML:CML + 128] = -C0
    c[0, CMR:CMR + 256] = np.arange(256) % 128
    c[1, CMR:CMR + 256] = 1
    c[0:64, CC0:CC0 + 64] = np.eye(64) - 1 / 64
    c[64:128, CC1:CC1 + 64] = np.eye(64) - 1 / 64
    return c


class Queues:

    def __init__(self, sem):
        self.sem = sem
        self.sems = {}
        self.value = {}
        self.lists = {e: [] for e in ("tensor", "vector", "scalar", "gpsimd", "sync")}

    def put(self, engine, make, waits=(), done=None, n=1):
        token = None
        if done:
            if done not in self.sems:
                self.sems[done] = self.sem(done)
                self.value[done] = 0
            self.value[done] += n
            token = (done, self.value[done])
        self.lists[engine].append((make, [w for w in waits if w], done, n))
        return token

    def run(self, name, engine):
        seen = {}
        for make, waits, done, n in self.lists[name]:
            need = {}
            for s, v in waits:
                if v > seen.get(s, 0):
                    need[s] = max(need.get(s, 0), v)
            for s, v in need.items():
                engine.wait_ge(self.sems[s], v)
                seen[s] = v
            last = make(engine)
            if done:
                last.then_inc(self.sems[done], n)


def build(nc, adj, adjt, xt, w1, w1bt, b1, w2, b2, w1g, b1g, w2g, b2g, wih, bih, whh, bhh, cst, out):
    ctx = ExitStack()
    with ctx:
        def sb(name, shape, dt=F32):
            return ctx.enter_context(nc.sbuf_tensor(name, shape, dt))

        q = Queues(lambda name: ctx.enter_context(nc.semaphore(name)))
        T = {}

        def put(*args, **kw):
            return q.put(*args, **kw)

        def tk(name, i):
            return T[name, i] if i >= 0 else None

        cs = sb("cs", [128, NC])
        idb = sb("idb", [128, 128], BF16)
        trx = sb("trx", [128, 128], BF16)
        tri = sb("tri", [128, 128], BF16)
        rst = sb("rst", [128, GB * 128], BF16)
        iot = sb("iot", [128, 128], BF16)
        mlr = sb("mlr", [2, 384], BF16)
        on3 = sb("on3", [128, 128], BF16)
        wuv = sb("wuv", [128, 2 * H + F])
        wa = sb("wa", [128, 2, H])
        wbt = sb("wbt", [128, 2, F])
        w2r = sb("w2r", [128, 2, F])
        w2c = sb("w2c", [128, 2, F])
        w2s = sb("w2s", [128, 2, F])
        b2r = sb("b2r", [3, F])
        wst = sb("wst", [128, 6])
        bs = sb("bs", [3, 2, H + F])
        bp = sb("bp", [3, 2, 3, H + F], BF16)
        be = sb("be", [3, 2, H + F])
        br = sb("br", [3, H + F], BF16)
        br2 = sb("br2", [3, GB, F], BF16)
        BD1 = sb("BD1", [128, 128])
        BD2 = sb("BD2", [128, 128])
        BDC = sb("BDC", [128, 128])
        BI = sb("BI", [128, 3, 128])
        BH = sb("BH", [128, 3, 128])
        gb = sb("gb", [128, 7])
        gbs = sb("gbs", [128, 2])

        A8 = [sb(f"A8{i}", [128, GB, 128]) for i in range(2)]
        AT = [sb(f"AT{i}", [128, GB, 128]) for i in range(3)]
        XT = [sb(f"XT{i}", [128, PG, 128]) for i in range(3)]
        M8 = sb("M8", [128, GB, 128], BF16)
        RK = sb("RK", [128, GB, 128], BF16)
        Q8 = [sb(f"Q8{i}", [128, GB, 128], BF16) for i in range(2)]
        CM = sb("CM", [128, GB, NTH])
        NV = sb("NV", [128, GB], BF16)
        N12 = [sb(f"N12{i}", [128, GB], BF16) for i in range(2)]
        VO = sb("VO", [128, NB])
        VE = sb("VE", [128, NB])
        NN = sb("NN", [128, NB])
        UA = [sb(f"UA{i}", [128, 2, 2 * H + F]) for i in range(3)]
        RU = [sb(f"RU{i}", [128, 2, H]) for i in range(2)]
        VP = [sb(f"VP{i}", [128, 2, 2, H], F16) for i in range(2)]
        UP = [sb(f"UP{i}", [128, 2, 2, H], F16) for i in range(2)]
        JK = sb("JK", [128, 2 * H])
        S2 = sb("S2", [128, NB])
        SS = sb("SS", [128, 2, 2, 128], BF16)
        OV = sb("OV", [128, 2, 128], BF16)
        GS = sb("GS", [128, 512], BF16)
        OK = [sb(f"OK{i}", [128, C1, 512], BF16) for i in range(2)]
        OK0 = [sb(f"OKX{i}", [128, C0 - C1, 256], BF16) for i in range(2)]
        OT = [sb(f"OT{i}", [128, 2, 128]) for i in range(2)]
        UV = [sb(f"UV{i}", [128, 2, H]) for i in range(2)]
        TA = [[sb(f"TA{i}{t}", [128, 2, 2, H]) for t in range(2)] for i in range(2)]
        TR = [sb(f"TR{i}", [128, 2, 2, H]) for i in range(RT)]
        TS = [sb(f"TS{i}", [128, 2, 3, H]) for i in range(2)]
        S = [sb(f"S{i}", [128, 2, H]) for i in range(2)]
        Z = [sb(f"Z{i}", [128, 2, H]) for i in range(2)]
        MT = [sb(f"MT{i}", [128, 2, 128]) for i in range(3)]
        ST = sb("ST", [128, 512])
        XR = [sb(f"XR{i}", [128, GB, F]) for i in range(2)]
        X1 = sb("X1", [128, GB, F])
        SQ = sb("SQ", [128, GB, F])
        st = sb("st", [128, 4, GB])
        XG = sb("XG", [128, PG, 128])
        M1 = sb("M1", [128, PG, 128])
        M2 = sb("M2", [128, GB, F])
        MS = sb("MS", [128, PG, 128])
        GR = sb("GR", [128, 512])
        GZ = sb("GZ", [128, 512])
        GN = sb("GN", [128, 512])
        GT = sb("GT", [128, 512])
        fb = sb("fb", [128, 3], BF16)
        fi = sb("fi", [1, 1], I32)
        Y = sb("Y", [128, GB, F])
        YO = sb("YO", [128, GB, F])
        PS = ctx.enter_context(nc.psum_tensor("PS", [128, 8, 512], F32))

        freed = {6: [], 7: []}
        held = set()

        def spare(n=1):
            while len(held) > 2 - n:
                yield

        def take(n=1):
            b = min(x for x in (6, 7) if x not in held)
            if n == 1 and turn[0] % 2 and not held:
                b = 7
            turn[0] += 1
            waits = [w for i in range(n) for w in freed[b + i]]
            held.update(range(b, b + n))
            return b, waits

        turn = [0]

        def release(b, token, n=1):
            for i in range(n):
                held.remove(b + i)
                freed[b + i] = [token]

        def dma(dst, src, done, waits=()):
            return put("sync", lambda e: e.dma_start(dst, src), waits, done, 16)

        for t in (BD1[:], BD2[:], BI[:], BH[:], wbt[:], w2r[:], bs[:]):
            t_ms = put("gpsimd", lambda e, t=t: e.memset(t, 0.0), (), "ms")
        t_ms = put("gpsimd", lambda e: e.memset(st[:, 3, :], -0.5), (), "ms")
        t_one = put("gpsimd", lambda e: e.memset(on3[:], 1.0), (), "ones")

        t_c = dma(cs[:], cst, "dc")
        def load(g):
            T["A8", g] = dma(A8[g % 2][:], adj[:, g * GB:(g + 1) * GB, :], f"dA{g % 2}", [tk("mask", g - 2)])
            T["XT", g] = dma(XT[g % 3][:], xt[:, g * PG:(g + 1) * PG, :], f"dY{g % 3}",
                             [tk("o0", PG * (g - 3) + PG - 1)])
            T["AT", g] = dma(AT[g % 3][:], adjt[:, g * GB:(g + 1) * GB, :], f"dT{g % 3}",
                             [tk("mt", PG * (g - 3) + PG - 1), tk("msg", g - 3)])

        load(0)
        for h in range(2):
            dma(wa[64 * h:64 * h + 64, 0, :], w1[0:F, :], "dw")
            dma(wa[64 * h:64 * h + 64, 1, :], w1[F:2 * F, :], "dw")
        dma(w2r[:, 0, :], w2[0:128, :], "dw", [t_ms])
        dma(w2r[0:64, 1, :], w2[128:H, :], "dw")
        dma(wbt[:, 0, :], w1bt[0:128, :], "dw")
        dma(wbt[0:64, 1, :], w1bt[128:H, :], "dw")
        dma(b2r[:], b2.rearrange("(a n) -> a n", a=1).to_broadcast([3, F]), "dw")
        dma(bs[:, 0, F:F + H], b1.rearrange("(a n) -> a n", a=1).to_broadcast([3, H]), "dw")
        t_w = dma(bs[:, 1, 0:F], b2g.rearrange("(a n) -> a n", a=1).to_broadcast([3, F]), "dw")

        for h in range(2):
            s = slice(64 * h, 64 * h + 64)
            dma(BD1[s, s], w1g, "dg")
            dma(BD2[s, s], w2g, "dg")
            for k in range(3):
                dma(BI[s, k, s], wih[:, 64 * k:64 * k + 64], "dg")
                dma(BH[s, k, s], whh[:, 64 * k:64 * k + 64], "dg")
                dma(gb[s, k:k + 1], bih[64 * k:64 * k + 64].rearrange("(p a) -> p a", a=1), "dg")
                dma(gb[s, 3 + k:4 + k], bhh[64 * k:64 * k + 64].rearrange("(p a) -> p a", a=1), "dg")
            t_g = dma(gb[s, 6:7], b1g.rearrange("(p a) -> p a", a=1), "dg")
        load(1)

        for d, s in ((idb[:], CI), (trx[:], CTX), (tri[:], CTI), (iot[:], CIO)):
            put("vector", lambda e, d=d, s=s: e.tensor_copy(d, cs[:, s:s + 128]), [t_c], "cb")
        put("vector", lambda e: e.tensor_copy(rst[:], cs[:, CRS:CRS + GB * 128]), [], "cb")
        put("vector", lambda e: e.tensor_copy(mlr[:], cs[0:2, CML:CML + 384]), [], "cb")
        put("vector", lambda e: e.tensor_copy(BDC[:, 0:64], cs[:, CC0:CC0 + 64]), [], "cb")
        t_cb = put("vector", lambda e: e.tensor_copy(BDC[:, 64:128], cs[:, CC1:CC1 + 64]), [], "cb")
        def ranks(g):
            i = g % 2
            T["mask", g] = put("vector", lambda e: e.tensor_scalar(M8[:], A8[i][:], 0.0, None, ALU.is_gt),
                               [T["A8", g], tk("q8", g - 1)], "mask")
            yield
            T["rk", g] = put("vector", lambda e: e.tensor_tensor_scan(
                RK[:].rearrange("p b n -> p (b n)"), rst[:], M8[:].rearrange("p b n -> p (b n)"), 0.0, ALU.mult, ALU.add),
                [T["mask", g], t_cb, tk("nn", g - 1)], "rk")
            yield
            T["q8", g] = put("vector", lambda e: e.tensor_tensor(Q8[i][:], M8[:], RK[:], ALU.mult),
                             [T["rk", g], tk("gp", PG * (g - 2) + PG - 1)], "q8")
            yield
            a = put("vector", lambda e: e.tensor_tensor(
                CM[:], RK[:, :, 127:128].to_broadcast([128, GB, NTH]),
                cs[:, CTH:CTH + NTH].unsqueeze(1).to_broadcast([128, GB, NTH]), ALU.is_gt),
                [T["rk", g]], "cm")

            def red(e):
                with nc.allow_low_precision(reason="counts up to 15"):
                    return e.tensor_reduce(NV[:], CM[:], AX.X, ALU.add)
            a = put("vector", red, [a, tk("off", g - 1)], "nv")
            yield
            T["n12", g] = put("vector", lambda e: e.tensor_scalar(N12[i][:], NV[:], float(C1), None, ALU.mult),
                              [a, tk("gp", PG * (g - 2) + PG - 1)], "n12")
            yield from spare()
            b, w = take()

            def off(e, b=b):
                e.matmul(PS[:, b, 0:GB], trx[:], NV[:], start=True, stop=True)
                return e.matmul(PS[:, b, GB:2 * GB], tri[:], NV[:], start=True, stop=True)
            T["off", g] = put("tensor", off, [a] + w, "off")
            s = slice(g * GB, (g + 1) * GB)
            t = put("vector", lambda e: e.scalar_tensor_tensor(
                NN[:, s], NV[:], float(C1), RK[:, :, 127], ALU.mult, ALU.subtract), [], "nn")
            T["nn", g] = put("vector", lambda e: e.tensor_scalar(NN[:, s], NN[:, s], float(C0), None, ALU.add), [t], "nn")
            put("vector", lambda e: e.tensor_scalar(VO[:, s], PS[:, b, 0:GB], -1.0, 0.5, ALU.mult, ALU.add), [T["off", g]], "vo")
            T["vo", g] = put("vector", lambda e: e.tensor_scalar(
                VE[:, s], PS[:, b, GB:2 * GB], -1.0, 0.5, ALU.mult, ALU.add), [], "vo")
            release(b, T["vo", g])

        def products(e, x, p, a):
            s = slice(64 * a, 64 * a + 64)
            e.matmul(PS[:, 6 + a, 0:2 * H + F], x[s, p % PG, :], wuv[s, :], start=True, stop=False)
            return e.matmul(PS[:, 6 + a, 0:H + F], on3[0:3, :], br[:], start=False, stop=True)

        def prep(p):
            g, j, i = p // PG, p % PG, p % 2
            gi = g % 2
            s2 = slice(2 * j, 2 * j + 2)
            for a in range(2):
                cc = slice(2 * p + a, 2 * p + a + 1)
                put("scalar", lambda e, a=a, cc=cc: e.activation(SS[:, 0, a, :], iot[:], ACT.Sign, bias=VO[:, cc]),
                    [T["vo", g], t_cb, tk("ov", p - 1)], "ss")
                t = put("scalar", lambda e, a=a, cc=cc: e.activation(SS[:, 1, a, :], iot[:], ACT.Sign, bias=VE[:, cc]),
                        [tk("gp", p - 1)], "ss")
            T["ss", p] = put("scalar", lambda e: e.activation(SS[:], SS[:], ACT.Relu), [t], "ss")
            yield
            t = put("scalar", lambda e: e.activation(MT[p % 3][:], AT[g % 3][:, s2, :], ACT.Sign),
                    [T["AT", g], tk("o0", p - 3)], "mt")
            T["mt", p] = put("scalar", lambda e: e.activation(MT[p % 3][:], MT[p % 3][:], ACT.Relu), [t], "mt")
            yield
            yield from spare(2)
            _, w = take(2)
            t = put("tensor", lambda e: products(e, XT[g % 3], p, 0), [T["XT", g], t_wu, t_wb, t_b, t_one] + w, "uvp")
            T["ov", p] = put("vector", lambda e: e.tensor_tensor(OV[:], SS[:, 0, :, :], SS[:, 1, :, :], ALU.subtract),
                             [T["ss", p], tk("gp", p - 1), tk("uvv", p - 1)], "ov")
            yield
            t = put("tensor", lambda e: products(e, XT[g % 3], p, 1), [], "uvp")
            put("scalar", lambda e: e.activation(UA[p % 3][:], PS[:, 6:8, 0:2 * H + F], ACT.Copy),
                [t, tk("mx0", p - 3), tk("o0", p - 3), tk("vp", p - 3), tk("up", p - 3), tk("s2", p - 3)], "u")
            put("scalar", lambda e: e.activation(VP[i][:, 0, :, :], PS[:, 6:8, H + F:2 * H + F], ACT.Copy), [tk("ga", p - 2)], "u")
            T["u", p] = put("scalar", lambda e: e.activation(UP[i][:, 0, :, :], PS[:, 6:8, F:H + F], ACT.Copy), [tk("uvv", p - 2)], "u")
            release(6, T["u", p], 2)
            yield
            T["vp", p] = put("vector", lambda e: e.tensor_tensor(
                VP[i][:, 1, :, :], UA[p % 3][:, :, H + F:2 * H + F], VP[i][:, 0, :, :], ALU.subtract), [T["u", p]], "vp")
            T["up", p] = put("gpsimd", lambda e: e.tensor_tensor(
                UP[i][:, 1, :, :], UA[p % 3][:, :, F:H + F], UP[i][:, 0, :, :], ALU.subtract), [T["u", p]], "up")
            for a in range(2):
                T["ru", p] = put("scalar", lambda e, a=a: e.activation(
                    RU[i][:, a, :], UA[p % 3][:, a, F:H + F], ACT.Relu, scale=NN[:, 2 * p + a:2 * p + a + 1]),
                    [T["u", p], tk("s0", p - 2), T["nn", g]], "ru")
            yield
            yield from spare(2)
            _, w = take(2)

            def gp(e):
                o = PS[:, 6, 0:256]
                e.matmul(o, mlr[0:2, 0:128], mlr[0:2, 128:384], start=True, stop=False)
                for a in range(2):
                    oa = PS[:, 6, 128 * a:128 * a + 128]
                    e.matmul(oa, Q8[gi][:, 2 * j + a, :], OV[:, a, :], start=False, stop=False)
                    e.matmul(oa, N12[gi][:, 2 * j + a:2 * j + a + 1].to_broadcast([128, 128]), SS[:, 1, a, :],
                             start=False, stop=(a == 1))
                for a in range(2):
                    e.transpose(pt[:, 128 * a:128 * a + 128], Q8[gi][:, 2 * j + a, :], idb[:])
                for a in range(2):
                    last = e.transpose(pt[:, 256 + 128 * a:384 + 128 * a], OV[:, a, :], idb[:])
                return last
            pt = PS[:, 7, 0:256].bitcast(BF16)
            T["gp", p] = put("tensor", gp, [T["q8", g], T["n12", g], T["ov", p]] + w, "gp")
            put("scalar", lambda e: e.activation(GS[:, 0:256], pt[:, 0:256], ACT.Copy), [T["gp", p], tk("ok", p - 1)], "gs")
            T["gs", p] = put("scalar", lambda e: e.activation(GS[:, 256:512], PS[:, 6, 0:256], ACT.Copy), [], "gs")
            T["otc", p] = put("scalar", lambda e: e.activation(
                OT[i][:].rearrange("p k n -> p (k n)"), pt[:, 256:512], ACT.Copy), [tk("st", p - 2)], "gs")
            release(6, T["otc", p], 2)
            yield
            for r in range(C1):
                T["ok", p] = put("vector", lambda e, r=r: e.tensor_scalar(OK[i][:, r, :], GS[:], float(r + 1), None, ALU.is_equal),
                                 [T["gs", p], tk("ga", p - 2)], "ok")
                if r % 2:
                    yield
            for a in range(2):
                T["s2"] = T["s2", p] = put("scalar", lambda e, a=a: e.activation(
                    JK[:], UA[p % 3][:, a, F:F + 2 * H], ACT.Square, accum_out=S2[:, 2 * p + a:2 * p + a + 1]),
                    [T.get("s2")], "s2")
            for r in range(C1, C0):
                T["ok", p] = put("vector", lambda e, r=r: e.tensor_scalar(
                    OK0[i][:, r - C1, :], GS[:, 0:256], float(r + 1), None, ALU.is_equal), [], "ok")
                if r % 2 == 0:
                    yield
            yield from spare()
            b, w = take()

            def uvv(e):
                for a in range(2):
                    for c in range(2):
                        last = e.matmul(PS[:, b, 256 * a:256 * a + H], OV[:, a, :], UP[i][:, c, a, :],
                                        start=(c == 0), stop=(c == 1))
                return last
            T["uvv", p] = put("tensor", uvv, [T["ov", p], T["u", p], T["up", p]] + w, "uvv")
            T["uv", p] = put("scalar", lambda e: e.activation(
                UV[i][:], PS[:, b, :].rearrange("p (k n) -> p k n", k=2)[:, :, 0:H], ACT.Copy),
                [T["uvv", p], tk("mx1", p - 2)], "uv")
            release(b, T["uv", p])

        count = [0]

        def quad(p, t, r, n):
            i, m = p % 2, count[0]
            count[0] += 1

            def gather(e):
                for a in range(2):
                    for s in range(n):
                        k = 256 * t + 128 * a
                        lhs = OK[i][:, r + s, k:k + 128] if r + s < C1 else OK0[i][:, r + s - C1, k:k + 128]
                        o = PS[:, 2 * (m % 3) + a, 256 * s:256 * s + H]
                        for c in range(2):
                            last = e.matmul(o, lhs, VP[i][:, c, a, :], start=(c == 0), stop=(c == 1))
                return last
            T["ga", p] = ga = put("tensor", gather, [T["ok", p], T["u", p], T["vp", p], tk("m", m - 3)], "ga")
            src = PS[:, 2 * (m % 3):2 * (m % 3) + 2, :].rearrange("p b (s n) -> p b s n", s=2)[:, :, 0:n, 0:H]
            u = (UV[i][:] if t else UA[p % 3][:, :, F:F + H]).unsqueeze(2).to_broadcast([128, 2, n, H])
            late = t == 0 and r + 3 >= C0
            if late:
                dst, w = TS[i][:, :, r + 3 - C0:r + 3 - C0 + n, :], tk("s0", p - 2)
            elif r == 0:
                dst, w = TA[i][t][:], tk(f"close{t}", p - 2)
            else:
                ring[0] += 1
                k = ring[0]
                dst, w = TR[k % RT][:], tk("add", k - RT)
            T[f"mx{t}", p] = T["m", m] = mx = put("vector", lambda e: e.tensor_tensor(dst, src, u, ALU.max),
                                                  [ga, T["uv" if t else "u", p], w], "max")
            if r and not late:
                T["acc", t, p] = T["add", k] = put("gpsimd", lambda e: e.tensor_tensor(
                    TA[i][t][:], TA[i][t][:], dst, ALU.add), [mx, T.get(("acc", t, p))], "add")

        ring = [-1]

        def own(p):
            i, g = p % 2, p // PG
            ts = TS[i]
            T["close0", p] = t = put("vector", lambda e: e.tensor_tensor(ts[:, :, 0:2, :], ts[:, :, 0:2, :], TA[i][0][:], ALU.add),
                                     [T["acc", 0, p], T["mx0", p]], "s0")
            yield
            t = put("vector", lambda e: e.tensor_tensor(S[i][:], ts[:, :, 0, :], ts[:, :, 1, :], ALU.add),
                    [t, tk("st", p - 2)], "s0")
            yield
            t = put("vector", lambda e: e.tensor_tensor(S[i][:], S[i][:], ts[:, :, 2, :], ALU.add), [t], "s0")
            T["s0", p] = put("vector", lambda e: e.tensor_tensor(S[i][:], S[i][:], RU[i][:], ALU.subtract),
                             [t, T["ru", p]], "s0")

        def tail(p, dense=False):
            g, j, i = p // PG, p % PG, p % 2
            if dense:
                t = T["s", p]
            else:
                yield
                T["close1", p] = t = put("vector", lambda e: e.tensor_tensor(
                    Z[i][:], TA[i][1][:, :, 0, :], TA[i][1][:, :, 1, :], ALU.add), [T["acc", 1, p], tk("st", p - 2)], "z")
                yield
            yield from spare()
            b, w = take()

            def stp(e, b=b):
                for a in range(2):
                    for o, k in ((PS[:, b, 128 * a:128 * a + 128], slice(0, 128)),
                                 (PS[0:64, b, 256 + 128 * a:384 + 128 * a], slice(128, H))):
                        last = e.matmul(o, S[i][:, a, k], cs[:, CI:CI + 128], start=True, stop=dense, is_transpose=True)
                        if not dense:
                            last = e.matmul(o, Z[i][:, a, k], OT[i][:, a, :], start=False, stop=True)
                return last
            T["st", p] = put("tensor", stp, [t, t_c] + ([] if dense else [T["s0", p], T["otc", p]]) + w, "st")
            put("scalar", lambda e, b=b: e.activation(ST[:, 0:256], PS[:, b, 0:256], ACT.Copy), [T["st", p], tk("o0", p - 1)], "stc")
            T["stc", p] = put("scalar", lambda e, b=b: e.activation(ST[0:64, 256:512], PS[0:64, b, 256:512], ACT.Copy), [], "stc")
            release(b, T["stc", p])
            yield
            yield from spare()
            b, w = take()

            def o0(e, a, b=b):
                o = PS[:, b, 64 * a:64 * a + 64]
                e.matmul(o, XT[g % 3][:, j, :], BDC[:, 64 * a:64 * a + 64], start=True, stop=False)
                e.matmul(o, MT[p % 3][:, a, :], UA[p % 3][:, a, 0:F], start=False, stop=False)
                e.matmul(o, ST[:, 128 * a:128 * a + 128], w2s[:, 0, :], start=False, stop=False)
                return e.matmul(o, ST[0:64, 256 + 128 * a:384 + 128 * a], w2s[0:64, 1, :], start=False, stop=True)
            put("tensor", lambda e: o0(e, 0), [T["stc", p], T["mt", p], T["u", p], t_w2, t_cb] + w, "o0")
            yield
            T["o0", p] = put("tensor", lambda e: o0(e, 1), [], "o0")
            T["xr", p] = put("scalar", lambda e, b=b: e.activation(
                XR[g % 2][:, 2 * j:2 * j + 2, :].rearrange("p a n -> p (a n)"), PS[:, b, 0:128], ACT.Copy),
                [T["o0", p], tk("x1", g - 2)], "xr")
            release(b, T["xr", p])

        def norm(src, dst, waits, done):
            a = put("scalar", lambda e: e.activation(SQ[:], src, ACT.Square), waits + [T.get("sq")], "sq")
            yield
            T["sq"] = a = put("vector", lambda e: e.tensor_reduce(st[:, 1, :], SQ[:], AX.X, ALU.add), [a, T.get("rs")], "ln")
            a = put("vector", lambda e: e.tensor_scalar(st[:, 2, :], st[:, 1, :], F * EPS, None, ALU.add), [a], "ln")
            a = put("gpsimd", lambda e: e.tensor_tensor(st[:, 2, :], st[:, 2, :], st[:, 3, :], ALU.pow), [a, t_ms], "pow")
            yield
            yield
            T[done] = T["rs"] = put("vector", lambda e: e.scalar_tensor_tensor(
                dst, src, F ** 0.5, st[:, 2, :].unsqueeze(2).to_broadcast([128, GB, F]), ALU.mult, ALU.mult), [a], "ln")

        def layer1(g, where=None):
            for _ in norm(XR[g % 2][:], X1[:], [T["xr", PG * g + PG - 1], tk("y", g - 1)], ("x1", g)):
                yield
            yield
            yield from spare()
            b, w = take()

            def xg(e, b=b):
                for k in range(PG):
                    last = e.transpose(PS[:, b, 128 * k:128 * k + 128],
                                       X1[:, 2 * k:2 * k + 2, :].rearrange("p a n -> p (a n)"), cs[:, CI:CI + 128])
                return last
            a = put("tensor", xg, [T["x1", g], t_c] + w, "xg")
            XGf = XG[:].rearrange("p k n -> p (k n)")
            T["xgc", g] = put("scalar", lambda e, b=b: e.activation(XGf, PS[:, b, :], ACT.Copy),
                              [a, tk("h", g - 1)], "xgc")
            release(b, T["xgc", g])
            yield
            yield from spare()
            b, w = take()
            a = put("tensor", lambda e, b=b: e.matmul(PS[:, b, :], BD1[:], XGf, start=True, stop=True),
                    [T["xgc", g], t_g] + w, "m1")
            a = put("scalar", lambda e, b=b: e.activation(M1[:].rearrange("p k n -> p (k n)"), PS[:, b, :], ACT.Relu,
                                                          bias=gb[:, 6:7]), [a, t_g], "m1c")
            release(b, a)
            yield
            yield from spare()
            b, w = take()

            def m2(e, b=b):
                e.matmul(PS[:, b, :], on3[0:3, :], br2[:].rearrange("p b n -> p (b n)"), start=True, stop=False)
                for k in range(PG):
                    last = e.matmul(PS[:, b, 128 * k:128 * k + 128], M1[:, k, :], BD2[:], start=False, stop=(k == PG - 1))
                return last
            a = put("tensor", m2, [a] + w, "m2")
            a = put("scalar", lambda e, b=b: e.activation(M2[:].rearrange("p b n -> p (b n)"), PS[:, b, :], ACT.Relu),
                    [a], "m2c")
            release(b, a)
            yield
            yield from spare()
            b, w = take()

            def msg(e, b=b):
                for k in range(GB):
                    s = slice(64 * (k % 2), 64 * (k % 2) + 64)
                    last = e.matmul(PS[s, b, 128 * (k // 2):128 * (k // 2) + 128], M2[:, k, :], AT[g % 3][:, k, :],
                                    start=True, stop=True)
                return last
            T["msg", g] = put("tensor", msg, [a, T["AT", g]] + w, "msg")
            MSf = MS[:].rearrange("p k n -> p (k n)")
            t_m = put("scalar", lambda e, b=b: e.activation(MSf, PS[:, b, :], ACT.Relu), [T["msg", g]], "msc")
            release(b, t_m)
            yield
            for k, dst in ((0, GR), (1, GZ)):
                yield from spare()
                b, w = take()

                put("tensor", lambda e, b=b, k=k: e.matmul(PS[:, b, :], BH[:, k, :], XGf, start=True, stop=False), w, "gate")
                yield
                a = put("tensor", lambda e, b=b, k=k: e.matmul(PS[:, b, :], BI[:, k, :], MSf, start=False, stop=True),
                        [t_m], "gate")
                a = put("scalar", lambda e, b=b, dst=dst, k=k: e.activation(dst[:], PS[:, b, :], ACT.Sigmoid,
                                                                            bias=gbs[:, k:k + 1]), [a, t_gb], "sig")
                release(b, a)
                if k == 0:
                    t_r = a
                else:
                    t_z = a
                yield
            yield from spare()
            b, w = take()
            a = put("tensor", lambda e, b=b: e.matmul(PS[:, b, :], BH[:, 2, :], XGf, start=True, stop=True), w, "gate")
            yield
            t = put("vector", lambda e, b=b: e.scalar_tensor_tensor(GT[:], PS[:, b, :], gb[:, 5:6], GR[:], ALU.add, ALU.mult),
                    [a, t_r, t_g], "gt")
            release(b, t)
            yield
            yield from spare()
            b, w = take()
            a = put("tensor", lambda e, b=b: e.matmul(PS[:, b, :], BI[:, 2, :], MSf, start=True, stop=True), w, "gate")
            yield
            t = put("vector", lambda e, b=b: e.tensor_tensor(GT[:], PS[:, b, :], GT[:], ALU.add), [a, t], "gt")
            release(b, t)
            yield
            t = put("scalar", lambda e: e.activation(GN[:], GT[:], ACT.Tanh, bias=gb[:, 2:3]), [t], "tanh")
            yield
            t = put("gpsimd", lambda e: e.tensor_tensor(GT[:], XGf, GN[:], ALU.subtract), [t], "gd")
            t = put("gpsimd", lambda e: e.tensor_tensor(GT[:], GT[:], GZ[:], ALU.mult), [t, t_z], "gd")
            yield
            t = T["h", g] = put("gpsimd", lambda e: e.tensor_tensor(GT[:], GT[:], GN[:], ALU.add), [t], "h")
            yield
            yield from spare()
            b, w = take()

            def yt(e, b=b):
                for k in range(PG):
                    last = e.matmul(PS[:, b, 128 * k:128 * k + 128], GT[:, 128 * k:128 * k + 128], BDC[:],
                                    start=True, stop=True)
                return last
            a = put("tensor", yt, [t] + w, "yt")
            yield
            T["y", g] = put("vector", lambda e, b=b: e.tensor_tensor(
                Y[:].rearrange("p b n -> p (b n)"), PS[:, b, :], X1[:].rearrange("p b n -> p (b n)"), ALU.add), [a], "y")
            release(b, T["y", g])
            yield
            for _ in norm(Y[:], YO[:], [T["y", g], tk("out", g - 1)], ("yo", g)):
                yield
            where = slice(g * GB, (g + 1) * GB) if where is None else where
            T["out", g] = dma(out[:, where, :], YO[:], "out", [T["yo", g]])

        def finish(gen):
            for k, _ in enumerate(gen):
                assert k < 99, "waits for a bank that nothing gives back"

        finish(ranks(0))

        put("vector", lambda e: e.tensor_scalar(wuv[:, F + H:F + 2 * H], wa[:, 1, :], SCALE, None, ALU.mult), [t_w], "wu")
        t = put("vector", lambda e: e.tensor_tensor(wuv[:, F:F + H], wa[:, 0, :], wa[:, 1, :], ALU.add), [], "wu")
        t_wu = put("vector", lambda e: e.tensor_scalar(wuv[:, F:F + H], wuv[:, F:F + H], SCALE, None, ALU.mult), [t], "wu")

        t = put("vector", lambda e: e.tensor_reduce(wst[:, 0:2], w2r[:], AX.X, ALU.add), [t_w], "wc")
        t = put("vector", lambda e: e.scalar_tensor_tensor(
            w2c[:], wst[:, 0:2].unsqueeze(2).to_broadcast([128, 2, F]), -1.0 / F, w2r[:], ALU.mult, ALU.add), [t], "wc")
        t_w2 = t = put("vector", lambda e: e.tensor_scalar(w2s[:], w2c[:], 1.0 / SCALE, None, ALU.mult), [t], "wc")
        t = put("vector", lambda e: e.tensor_reduce(wst[0:3, 2:3], b2r[:], AX.X, ALU.add), [], "wc")
        t = put("vector", lambda e: e.scalar_tensor_tensor(
            bs[:, 0, 0:F], wst[0:3, 2:3].to_broadcast([3, F]), -1.0 / F, b2r[:], ALU.mult, ALU.add), [t, t_ms], "wc")

        t = put("vector", lambda e: e.tensor_scalar(bs[:, 0, F:F + H], bs[:, 0, F:F + H], SCALE, None, ALU.mult), [t], "wc")
        w = [t]
        for i in range(3):
            src = bs if i == 0 else be
            t = put("vector", lambda e, i=i, src=src: e.tensor_copy(bp[:, :, i, :], src[:]), w, "bp")
            if i < 2:
                t = put("vector", lambda e, i=i, src=src: e.tensor_tensor(be[:], src[:], bp[:, :, i, :], ALU.subtract),
                        [t], "bp")
            w = [t]
        for i in range(3):
            sel = cs[0:3, CSL + i:CSL + i + 1]
            if i == 0:
                t = put("vector", lambda e, i=i, sel=sel: e.tensor_scalar(be[:], bp[:, :, i, :], sel, None, ALU.mult),
                        [t_c] + w, "bp")
            else:
                t = put("vector", lambda e, i=i, sel=sel: e.scalar_tensor_tensor(
                    be[:], bp[:, :, i, :], sel, be[:], ALU.mult, ALU.add), [t], "bp")
        put("vector", lambda e: e.tensor_copy(br[:], be[:, 0, :]), [t], "bp")
        t_b = put("vector", lambda e: e.tensor_copy(
            br2[:], be[:, 1, 0:F].unsqueeze(1).to_broadcast([3, GB, F])), [], "bp")

        b, w = take()

        def ww(e, b=b):
            for h in range(2):
                s = slice(64 * h, 64 * h + 64)
                e.matmul(PS[s, b, 0:F], wbt[:, 0, :], w2c[:, 0, :], start=True, stop=False)
                last = e.matmul(PS[s, b, 0:F], wbt[:, 1, :], w2c[:, 1, :], start=False, stop=True)
            return last
        t_ww = put("tensor", ww, [t_w, t_w2] + w, "ww")
        t_wb = put("vector", lambda e, b=b: e.tensor_scalar(wuv[:, 0:F], PS[:, b, 0:F], -1.0, None, ALU.mult),
                   [t_ww], "wb")
        release(b, t_wb)

        finish(prep(0))
        t_gb = put("vector", lambda e: e.tensor_tensor(gbs[:], gb[:, 0:2], gb[:, 3:5], ALU.add), [t_g], "gbs")
        parts = [(0, r, min(2, C0 - r)) for r in range(0, C0, 2)] + [(1, r, 2) for r in range(0, C1, 2)]
        started = [False] * NG
        link = dict.fromkeys("prtdo", iter(()))
        for p in range(NP):
            g, j = p // PG, p % PG
            link["p"] = prep(p + 1) if p + 1 < NP else iter(())
            link["t"] = tail(p - 1) if p else iter(())
            if j == 0 and g and g + 1 < NG:
                load(g + 1)
            if j == 0 and g + 1 < NG:
                link["r"] = ranks(g + 1)
            for n, (t, r, k) in enumerate(parts):
                quad(p, t, r, k)
                if (t, r) == (0, C0 - 1):
                    finish(link["o"])
                    link["o"] = own(p)
                for c in ORDER[j][n]:
                    if next(link[c], 0) == 0 and c == "t" and j == 0 and g and not started[g - 1]:
                        started[g - 1] = True
                        finish(link["d"])
                        link["d"] = layer1(g - 1)
            finish(link["p"])
            finish(link["t"])
            if j == 0 and g and not started[g - 1]:
                started[g - 1] = True
                finish(link["d"])
                link["d"] = layer1(g - 1)
        finish(link["d"])
        finish(link["o"])
        finish(tail(NP - 1))
        finish(layer1(NG - 1))

        put("vector", lambda e: e.tensor_reduce(st[:, 0, 0:1], VE[:], AX.X, ALU.min), [T["yo", NG - 1]], "flag")
        put("vector", lambda e: e.tensor_reduce(st[:, 0, 1:2], S2[:], AX.X, ALU.max), [T["s2", NP - 1]], "flag")
        a = put("vector", lambda e: e.tensor_reduce(st[:, 0, 2:3], S2[:], AX.X, ALU.min), [], "flag")
        put("vector", lambda e: e.tensor_scalar(fb[:, 0:1], st[:, 0, 0:1], 0.5 - LIMIT, None, ALU.is_lt), [a], "flag")
        put("vector", lambda e: e.tensor_scalar(fb[:, 1:2], st[:, 0, 1:2], MOST, None, ALU.is_gt), [], "flag")
        a = put("vector", lambda e: e.tensor_scalar(fb[:, 2:3], st[:, 0, 2:3], LEAST, None, ALU.is_lt), [], "flag")

        def total(e):
            for k in range(3):
                last = e.matmul(PS[0:1, 6, 0:1], fb[:, k:k + 1], on3[:, 0:1], start=(k == 0), stop=(k == 2))
            return last
        a = put("tensor", total, [a] + freed[6], "fsum")
        a = put("vector", lambda e: e.tensor_copy(fi[:], PS[0:1, 6, 0:1]), [a], "flag")

        def emit(q):
            with nc.Block() as block:
                @block.tensor
                def _(e):
                    q.run("tensor", e)

                @block.vector
                def _(e):
                    q.run("vector", e)

                @block.scalar
                def _(e):
                    q.run("scalar", e)

                @block.gpsimd
                def _(e):
                    q.run("gpsimd", e)

                @block.sync
                def _(e):
                    q.run("sync", e)
                    e.wait_ge(q.sems["out"], q.value["out"])
                    if "flag" in q.sems:
                        e.wait_ge(q.sems["flag"], q.value["flag"])

        emit(q)

        over = nc.values_load(fi[:], min_val=0, max_val=384)
        with nc.If(over > 0):
            with nc.Fori(0, NG) as gv:
                q = Queues(lambda name: ctx.enter_context(nc.semaphore("g_" + name)))
                T.clear()
                freed.update({6: [], 7: []})
                t_one = t_wu = t_b = t_wb = t_c = t_g = t_gb = t_ms = t_w2 = t_cb = None
                here = bass.ds(gv * GB, GB)
                T["A8", 0] = dma(A8[0][:], adj[:, here, :], "dA")
                T["AT", 0] = dma(AT[0][:], adjt[:, here, :], "dT")
                T["XT", 0] = dma(XT[0][:], xt[:, bass.ds(gv * PG, PG), :], "dY")
                t_mk = put("vector", lambda e: e.tensor_scalar(A8[0][:], A8[0][:], 0.0, None, ALU.is_gt), [T["A8", 0]], "mask")
                m = 0
                t_z = None
                for p in range(PG):
                    i = p % 2
                    a = put("tensor", lambda e, p=p: (products(e, XT[0], p, 0), products(e, XT[0], p, 1))[1],
                            [T["XT", 0], tk("u", p - 1)] + freed[6] + freed[7], "uvp")
                    put("scalar", lambda e, p=p: e.activation(UA[p % 3][:, :, 0:H + F], PS[:, 6:8, 0:H + F], ACT.Copy),
                        [a, tk("s", p - 3), tk("o0", p - 3)], "u")
                    T["u", p] = put("scalar", lambda e: e.activation(RU[0][:], PS[:, 6:8, H + F:2 * H + F], ACT.Copy),
                                    [tk("ga", p - 1)], "u")
                    freed.update({6: [T["u", p]], 7: [T["u", p]]})
                    T["mt", p] = put("gpsimd", lambda e, p=p: e.tensor_scalar(
                        MT[p % 3][:], AT[0][:, 2 * p:2 * p + 2, :], 0.0, None, ALU.is_gt), [T["AT", 0], tk("o0", p - 3)], "mt")
                    for a in range(2):
                        for r in range(32):
                            def spread(e, a=a, r=r, m=m):
                                for s in range(4):
                                    k = 4 * r + s
                                    last = e.matmul(PS[:, 2 * (m % 2) + s // 2, 256 * (s % 2):256 * (s % 2) + H],
                                                    cs[:, CI + k:CI + k + 1].to_broadcast([128, 128]), RU[0][:, a, :],
                                                    start=True, stop=True)
                                return last
                            T["ga", p] = ga = put("tensor", spread, [T["u", p], tk("m", m - 2)], "ga")
                            src = PS[:, 2 * (m % 2):2 * (m % 2) + 2, :].rearrange("p b (s n) -> p (b s) n", s=2)[:, :, 0:H]
                            t = TR[0][:].rearrange("p a s n -> p (a s) n")
                            w = T["m", m] = put("vector", lambda e, t=t, src=src, a=a, p=p: e.tensor_tensor(
                                t, src, UA[p % 3][:, a:a + 1, F:F + H].to_broadcast([128, 4, H]), ALU.max), [ga, T["u", p], t_z], "max")
                            w = put("vector", lambda e, t=t, a=a, p=p, r=r: e.tensor_tensor(
                                t, t, A8[0][:, 2 * p + a, 4 * r:4 * r + 4].unsqueeze(2).to_broadcast([128, 4, H]), ALU.mult),
                                [w, t_mk], "md")
                            dst = S[i][:, a, :] if r == 0 else TS[0][:, 0, 0, :]
                            w = put("vector", lambda e, t=t, dst=dst: e.tensor_reduce(
                                dst, t.rearrange("p s n -> p n s"), AX.X, ALU.add), [w, tk("st", p - 2)], "rd")
                            if r:
                                w = put("vector", lambda e, i=i, a=a: e.tensor_tensor(
                                    S[i][:, a, :], S[i][:, a, :], TS[0][:, 0, 0, :], ALU.add), [w], "z")
                            T["s", p] = t_z = w
                            m += 1
                    finish(tail(p, dense=True))
                finish(layer1(0, here))
                emit(q)
                for s in q.sems.values():
                    nc.gpsimd.sem_clear(s)
                nc.all_engine_barrier()


def kernel(x, adj, L0_gnn_W1, L0_gnn_b1, L0_gnn_W2, L0_gnn_b2, L1_gnn_W1, L1_gnn_b1, L1_gnn_W2, L1_gnn_b2,
           L1_gnn_W_ih, L1_gnn_b_ih, L1_gnn_W_hh, L1_gnn_b_hh):
    import concourse.bacc as _bacc
    from concourse.bass_utils import run_bass_kernel_spmd as _run

    x, adj = np.asarray(x), np.asarray(adj)
    w1 = np.asarray(L0_gnn_W1)
    arrays = {
        "adj": adj.transpose(1, 0, 2),
        "adjt": adj.transpose(2, 0, 1),
        "xt": x.reshape(NP, 2, N, F).transpose(1, 3, 0, 2).reshape(2 * F, NP, N),
        "w1": w1,
        "w1bt": w1[F:].T,
        "b1": L0_gnn_b1,
        "w2": L0_gnn_W2,
        "b2": L0_gnn_b2,
        "w1g": L1_gnn_W1,
        "b1g": L1_gnn_b1,
        "w2g": L1_gnn_W2,
        "b2g": L1_gnn_b2,
        "wih": np.asarray(L1_gnn_W_ih).T,
        "bih": L1_gnn_b_ih,
        "whh": np.asarray(L1_gnn_W_hh).T,
        "bhh": L1_gnn_b_hh,
        "cst": constants(),
    }
    nc = _bacc.Bacc("TRN2", target_bir_lowering=False, num_devices=1)
    feeds, args = {}, []
    for name, a in arrays.items():
        a = np.ascontiguousarray(a)
        feeds[f"in_{name}"] = a
        args.append(nc.dram_tensor(f"in_{name}", a.shape, mybir.dt.from_np(a.dtype), kind="ExternalInput").ap())
    out = nc.dram_tensor("out_0", (N, NB, F), F32, kind="ExternalOutput").ap()
    build(nc, *args, out)
    r = _run(nc, [feeds], core_ids=[0])
    return np.ascontiguousarray(r.results[0]["out_0"].transpose(1, 0, 2))
```
